# Optimizing a Trainium2 kernel written in Bass

```python
import numpy as np
import jax
import jax.numpy as jnp

def _softmax(x, axis=-1):
    return jax.nn.softmax(x, axis=axis)

def _gelu(x):
    return jax.nn.gelu(x, approximate=True)

def _silu(x):
    return jax.nn.silu(x)

def _sigmoid(x):
    return jax.nn.sigmoid(x)

def _layernorm(x, axis=-1, eps=1e-05):
    m = jnp.mean(x, axis=axis, keepdims=True)
    v = jnp.var(x, axis=axis, keepdims=True)
    return (x - m) / jnp.sqrt(v + eps)

def _scatter_add(tgt, idx, src, axis=0):
    return tgt.at[idx].add(src)

def _segment_sum(src, seg, n):
    return jax.ops.segment_sum(src, seg, n)
kernel_name = 'mk_flamingo_gated_d1_seqx_r8_90763a'

def setup_inputs(seed: int=0):
    np.random.seed(seed)
    _w = jnp.asarray

    def _rec_inputs():
        import jax
        import jax.numpy as jnp
        _rk = jax.random.key(seed)
        x = -0.0002928 + 1 * jax.random.normal(jax.random.fold_in(_rk, 1), (8, 128, 256), jnp.float32)
        _lenS = 128 - jax.random.randint(jax.random.fold_in(_rk, 7), (8,), 0, max(1, 128 // 4) + 1, jnp.int32)
        _lenS2 = 128 - jax.random.randint(jax.random.fold_in(_rk, 8), (8,), 0, max(1, 128 // 4) + 1, jnp.int32)
        _ctx_2048P = jax.random.normal(jax.random.fold_in(_rk, 11), (8, 16, 256), jnp.float32)
        _ctx_2048c = jax.random.dirichlet(jax.random.fold_in(_rk, 511), 0.3 * jnp.ones((16,), jnp.float32), (8, 128))
        _ctx_2048t = jnp.einsum('bsk,bkd->bsd', _ctx_2048c, _ctx_2048P)
        _ctx_2048t = _ctx_2048t * jax.lax.rsqrt(jnp.mean(jnp.square(_ctx_2048t)) + 1e-12) * 0.953939
        ctx_2048 = -1.39393e-06 + 0.999914 * (_ctx_2048t + 0.3 * jax.random.normal(jax.random.fold_in(_rk, 611), (8, 128, 256), jnp.float32))
        _g = jax.random.normal(jax.random.fold_in(_rk, 9001), (2, 1), jnp.float32)
        _g = jnp.sign(_g) * jnp.maximum(jnp.abs(_g), 1.0) + (_g == 0) * 1.0
        g_xattn = _g[0]
        g_ffn = _g[1]
        return (x, ctx_2048, g_xattn, g_ffn)
    x, ctx_2048, g_xattn, g_ffn = _rec_inputs()

    def _L0_xattn_setup():
        import jax, jax.numpy as jnp
        import numpy as np
        B, S, E, NH = (2, 128, 256, 16)
        DH = E // NH
        EPS = 1e-06

        def _mlstm_forward(q, k, v, Wi, bi, Wf, bf, ln_scale):
            b, s, e = q.shape
            nh = Wi.shape[1]
            dh = e // nh
            x = jnp.concatenate([q, k, v], axis=-1)
            ig = (x @ Wi + bi).transpose(0, 2, 1)[..., None]
            fg = (x @ Wf + bf).transpose(0, 2, 1)[..., None]
            split = lambda t: t.reshape(b, s, nh, dh).transpose(0, 2, 1, 3)
            qh, kh, vh = (split(q), split(k), split(v))
            log_f = jax.nn.log_sigmoid(fg)
            log_f_cum = jnp.concatenate([jnp.zeros((b, nh, 1, 1), q.dtype), jnp.cumsum(log_f, axis=2)], axis=2)
            fg_mat = log_f_cum - jnp.transpose(log_f_cum, (0, 1, 3, 2))
            ltr = jnp.tril(jnp.ones((s, s), dtype=bool))
            log_fg = jnp.where(ltr, fg_mat[:, :, 1:, 1:], -jnp.inf)
            log_D = log_fg + jnp.transpose(ig, (0, 1, 3, 2))
            max_log_D = jnp.max(log_D, axis=-1, keepdims=True)
            D = jnp.exp(log_D - max_log_D)
            qk = jnp.einsum('bhsd,bhtd->bhst', qh, kh) / jnp.sqrt(jnp.asarray(dh, q.dtype))
            C = qk * D
            normalizer = jnp.maximum(jnp.abs(C.sum(-1, keepdims=True)), jnp.exp(-max_log_D))
            Cn = C / (normalizer + EPS)
            h = jnp.einsum('bhst,bhtd->bhsd', Cn, vh)
            mu = h.mean(-1, keepdims=True)
            var = ((h - mu) ** 2).mean(-1, keepdims=True)
            hn = (h - mu) * jax.lax.rsqrt(var + EPS)
            hn = hn * ln_scale.reshape(1, nh, 1, dh)
            return hn.transpose(0, 2, 1, 3).reshape(b, s, e)
        key = jax.random.key(seed)
        ks = jax.random.split(key, 6)
        q = jax.random.normal(ks[0], (B, S, E), dtype=jnp.float32)
        k = jax.random.normal(ks[1], (B, S, E), dtype=jnp.float32)
        v = jax.random.normal(ks[2], (B, S, E), dtype=jnp.float32)
        Wi = jax.random.normal(ks[3], (3 * E, NH), dtype=jnp.float32) * 0.02
        bi = jax.random.normal(ks[4], (NH,), dtype=jnp.float32) * 0.1
        Wf = jax.random.normal(ks[5], (3 * E, NH), dtype=jnp.float32) * 0.02
        bf = jnp.linspace(3.0, 6.0, NH, dtype=jnp.float32)
        ln_scale = jnp.ones((E,), dtype=jnp.float32)
        return {'q': q, 'k': k, 'v': v, 'Wi': Wi, 'bi': bi, 'Wf': Wf, 'bf': bf, 'ln_scale': ln_scale}
    _L0_xattn_all = _L0_xattn_setup()
    _L0_xattn_in = {k: v for k, v in _L0_xattn_all.items() if k in ('Wi', 'bi', 'Wf', 'bf', 'ln_scale')}
    del _L0_xattn_all

    def _L0_ffn_setup():
        import jax, jax.numpy as jnp
        import numpy as np
        E, TOPK, H, I = (8, 2, 256, 512)
        SOFTCAP = 30.0
        key = jax.random.key(seed)
        ks = jax.random.split(key, 5)
        s = 1.0 / np.sqrt(H)
        si = 1.0 / np.sqrt(I)
        return {'hidden_states': jax.random.normal(ks[0], (4, 256, H), jnp.float32), 'w_gate': jax.random.normal(ks[1], (H, E), jnp.float32) * s, 'w1': jax.random.normal(ks[2], (E, H, I), jnp.float32) * s, 'w3': jax.random.normal(ks[3], (E, H, I), jnp.float32) * s, 'w2': jax.random.normal(ks[4], (E, I, H), jnp.float32) * si}
    _L0_ffn_all = _L0_ffn_setup()
    _L0_ffn_in = {k: v for k, v in _L0_ffn_all.items() if k in ('w_gate', 'w1', 'w3', 'w2')}
    del _L0_ffn_all
    return {'x': x, 'ctx_2048': ctx_2048, 'g_xattn': g_xattn, 'g_ffn': g_ffn, 'L0_xattn_Wi': _L0_xattn_in['Wi'], 'L0_xattn_bi': _L0_xattn_in['bi'], 'L0_xattn_Wf': _L0_xattn_in['Wf'], 'L0_xattn_bf': _L0_xattn_in['bf'], 'L0_xattn_ln_scale': _L0_xattn_in['ln_scale'], 'L0_ffn_w_gate': _L0_ffn_in['w_gate'], 'L0_ffn_w1': _L0_ffn_in['w1'], 'L0_ffn_w3': _L0_ffn_in['w3'], 'L0_ffn_w2': _L0_ffn_in['w2']}

def reference(x, ctx_2048, g_xattn, g_ffn, L0_xattn_Wi, L0_xattn_bi, L0_xattn_Wf, L0_xattn_bf, L0_xattn_ln_scale, L0_ffn_w_gate, L0_ffn_w1, L0_ffn_w3, L0_ffn_w2):
    import jax
    import jax.numpy as jnp

    def _L0_xattn_ref(q, k, v, Wi, bi, Wf, bf, ln_scale):
        import jax, jax.numpy as jnp
        import numpy as np
        B, S, E, NH = (2, 128, 256, 16)
        DH = E // NH
        EPS = 1e-06

        def _mlstm_forward(q, k, v, Wi, bi, Wf, bf, ln_scale):
            b, s, e = q.shape
            nh = Wi.shape[1]
            dh = e // nh
            x = jnp.concatenate([q, k, v], axis=-1)
            ig = (x @ Wi + bi).transpose(0, 2, 1)[..., None]
            fg = (x @ Wf + bf).transpose(0, 2, 1)[..., None]
            split = lambda t: t.reshape(b, s, nh, dh).transpose(0, 2, 1, 3)
            qh, kh, vh = (split(q), split(k), split(v))
            log_f = jax.nn.log_sigmoid(fg)
            log_f_cum = jnp.concatenate([jnp.zeros((b, nh, 1, 1), q.dtype), jnp.cumsum(log_f, axis=2)], axis=2)
            fg_mat = log_f_cum - jnp.transpose(log_f_cum, (0, 1, 3, 2))
            ltr = jnp.tril(jnp.ones((s, s), dtype=bool))
            log_fg = jnp.where(ltr, fg_mat[:, :, 1:, 1:], -jnp.inf)
            log_D = log_fg + jnp.transpose(ig, (0, 1, 3, 2))
            max_log_D = jnp.max(log_D, axis=-1, keepdims=True)
            D = jnp.exp(log_D - max_log_D)
            qk = jnp.einsum('bhsd,bhtd->bhst', qh, kh) / jnp.sqrt(jnp.asarray(dh, q.dtype))
            C = qk * D
            normalizer = jnp.maximum(jnp.abs(C.sum(-1, keepdims=True)), jnp.exp(-max_log_D))
            Cn = C / (normalizer + EPS)
            h = jnp.einsum('bhst,bhtd->bhsd', Cn, vh)
            mu = h.mean(-1, keepdims=True)
            var = ((h - mu) ** 2).mean(-1, keepdims=True)
            hn = (h - mu) * jax.lax.rsqrt(var + EPS)
            hn = hn * ln_scale.reshape(1, nh, 1, dh)
            return hn.transpose(0, 2, 1, 3).reshape(b, s, e)
        return _mlstm_forward(q, k, v, Wi, bi, Wf, bf, ln_scale)

    def _L0_ffn_ref(hidden_states, w_gate, w1, w3, w2):
        import jax, jax.numpy as jnp
        import numpy as np
        E, TOPK, H, I = (8, 2, 256, 512)
        SOFTCAP = 30.0
        orig_shape = hidden_states.shape
        x = hidden_states.reshape(-1, H)
        logits = x @ w_gate
        logits = SOFTCAP * jnp.tanh(logits / SOFTCAP)
        probs = jax.nn.softmax(logits, axis=-1)
        _, idx = jax.lax.top_k(probs, TOPK)
        mask = jax.nn.one_hot(idx, E, dtype=probs.dtype).sum(-2)
        weights = probs * mask
        out = jnp.zeros_like(x)
        for e in range(E):
            h = jax.nn.silu(x @ w1[e]) * (x @ w3[e])
            out = out + h @ w2[e] * weights[:, e:e + 1]
        return out.reshape(orig_shape)
    x = x + jnp.tanh(g_xattn[0]) * _L0_xattn_ref(_layernorm(x, axis=-1), ctx_2048, ctx_2048, L0_xattn_Wi, L0_xattn_bi, L0_xattn_Wf, L0_xattn_bf, L0_xattn_ln_scale)
    x = x + jnp.tanh(g_ffn[0]) * _L0_ffn_ref(_layernorm(x, axis=-1), L0_ffn_w_gate, L0_ffn_w1, L0_ffn_w3, L0_ffn_w2)
    return x

_drawn_inputs = setup_inputs


def setup_inputs(seed=0):
    import zlib

    import numpy as np

    out = dict(_drawn_inputs(seed))
    spreads = {'L0_xattn_ln_scale': (1.0, 0.2)}
    factors = {'L0_xattn_bi': 64.0, 'L0_xattn_Wf': 3.373}
    for name, (base, spread) in spreads.items():
        noise = np.random.default_rng([zlib.crc32(name.encode()), seed]).standard_normal(out[name].shape)
        drawn = base * np.exp(spread * noise) if base else spread * noise
        out[name] = jnp.asarray(drawn.astype(out[name].dtype))
    for name, factor in factors.items():
        out[name] = (out[name] * factor).astype(out[name].dtype)
    return out
```

```python
from contextlib import ExitStack

import concourse.bass as bass
from concourse import mybir

F32 = mybir.dt.float32
BF16 = mybir.dt.bfloat16
I32 = mybir.dt.int32
ALU = mybir.AluOpType
ACT = mybir.ActivationFunctionType
AX_X = mybir.AxisListType.X

P = 128
BIG = 1.0e30
LN_EPS = 1e-5
MLSTM_EPS = 1e-6
SOFTCAP = 30.0
RSQRT_MAGIC = 0x5F3759DF


def bass_gated_mlstm_moe_kernel(nc, x, ctx_in, g_xattn, g_ffn, wi, bi, wf, bf, ln_scale, w_gate, w1, w3, w2, out):
    B, S, H = x.shape
    NH = wi.shape[1]
    DH = H // NH
    KC = H // P
    E = w_gate.shape[1]
    I = w1.shape[2]
    IC = I // P
    T = B * S
    TOPK = 2
    HC = NH // KC
    VW = 32
    NT = TOPK * T // P + E - 1
    assert S == P and NT % 2 == 1 and (NT - 1) * P <= TOPK * T + E * (P - 1) < (NT + 1) * P
    G2 = 2 * NH
    BH = B * NH
    SEL = 6
    WE = 2 * KC * I + IC * H

    mprime_dram = nc.dram_tensor("mprime_scratch", [B, NH * S], F32, kind="Internal").ap()
    xn_dram = nc.dram_tensor("xnorm_scratch", [T, H], F32, kind="Internal").ap()

    with ExitStack() as ctx:
        def sb(name, shape, dt=F32):
            return ctx.enter_context(nc.sbuf_tensor(name, shape, dt))

        def sem(name):
            return ctx.enter_context(nc.semaphore(name))

        bank = [ctx.enter_context(nc.psum_tensor(f"bank{i}", [P, 2, 512] if i < 2 else [P, 512], F32)) for i in range(6)]
        ps_scores = bank[0:2]
        ps_ht = bank[2]
        ps_h = bank[3]
        ps_tr = bank[4]
        ps_small = bank[5]

        w_sb = sb("w_sb", [P, E * WE])
        x_sb = sb("x_sb", [P, B, H])
        ctx_sb = sb("ctx_sb", [P, B, H])
        xn_sb = sb("xn_sb", [P, B, H])
        qkT = sb("qkT", [P, B, 2 * KC, S])
        qbd = sb("qbd", [P, 2, KC, HC, S])
        dec = sb("dec", [P, 3, NH, S])
        vp = sb("vp", [P, 2, NH, VW])
        wg_sb = sb("wg_sb", [P, 3 * KC, G2])
        gb_sb = sb("gb_sb", [P, G2])
        wr_sb = sb("wr_sb", [P, KC, E])
        lns = sb("lns", [P, H])
        gx = sb("gx", [P, 2])
        tg = sb("tg", [P, 2])
        ident = sb("ident", [P, P])
        tri = sb("tri", [P, P])
        ones = sb("ones", [P, P])
        tri_s = sb("tri_s", [P, P], BF16)
        ones_b = sb("ones_b", [P, P], BF16)
        iota_r = sb("iota_r", [P, P])
        iota_t = sb("iota_t", [P, NT])
        iota_c = sb("iota_c", [P, E])
        iota_e = sb("iota_e", [P, E])
        tok_p = sb("tok_p", [P, 1])
        tok_j = sb("tok_j", [P, B])
        dump = sb("dump", [P, 1])
        one_c = sb("one_c", [P, 1])
        zrow = sb("zrow", [P, H])

        st = sb("st", [P, B, 6])
        mv = sb("mv", [P, B, 2])
        gates = sb("gates", [P, B, 2, NH])
        fa = sb("fa", [P, BH])
        fu = sb("fu", [P, BH])
        fl = sb("fl", [P, BH])
        logf = sb("logf", [P, BH])
        fcum = sb("fcum", [P, BH])
        amat = sb("amat", [P, BH])
        aT = sb("aT", [P, S])
        mT = sb("mT", [P, S])
        mlog = sb("mlog", [P, BH])
        floor = sb("floor", [P, BH])
        cvT = sb("cvT", [P, 512])
        hh = sb("hh", [P, NH, DH])
        hc = sb("hc", [P, NH, DH])
        hq = sb("hq", [P, NH, DH])
        s16 = sb("s16", [P, 8, NH])
        rs = sb("rs", [P, 4, NH])
        xlT = sb("xlT", [P, H])

        lt = sb("lt", [P, B, E])
        ex = sb("ex", [P, B, E])
        ex2 = sb("ex2", [P, B, E])
        key = sb("key", [P, B, E])
        oh = sb("oh", [P, TOPK, B, E])
        r8 = sb("r8", [P, 8, B])
        wsel = sb("wsel", [P, TOPK, B])
        mask = sb("mask", [P, B, E], BF16)
        cnt = sb("cnt", [P, E])
        ctile = sb("ctile", [P, E, E])
        ntile = sb("ntile", [P, E])
        zero8 = sb("zero8", [P, E])
        etile = sb("etile", [P, E])
        base = sb("base", [P, E])
        slotm = sb("slotm", [P, B, E])
        slotk = sb("slotk", [P, TOPK, B, E])
        slotf = sb("slotf", [P, TOPK * B])
        sloti = sb("sloti", [P, 3, TOPK * B], I32)
        srf = sb("srf", [P, 2, TOPK * B])
        wpart = sb("wpart", [P, 3, TOPK * B], BF16)
        wres = sb("wres", [P, 2, TOPK * B])
        tab = sb("tab", [P, SEL, NT])
        tokf = sb("tokf", [P, 2, NT])
        gidx = sb("gidx", [P, NT], I32)
        sidx = sb("sidx", [P, NT], I32)
        wslot = sb("wslot", [P, NT + 1])
        etf = sb("etf", [P, NT])
        eti = sb("eti", [P, NT], I32)

        dflat = dec.rearrange("p a h s -> p (a h s)")
        cflat = ctx_sb.rearrange("p b h -> p (b h)")

        qflat = qbd.rearrange("p a c h s -> p (a c h s)")

        def carve(flat, widths):
            at, got = 0, []
            for w in widths:
                got.append(flat[:, at:at + w])
                at += w
            return got

        *tail, = carve(dflat, [I] * 6)
        sg_sb, h_sb, hT_sb = tail[0:2], tail[2:4], tail[4:6]
        xg_sb = carve(cflat, [H] * 8)
        xg_sb, xT_sb, y_sb = xg_sb[0:3], xg_sb[3:5], xg_sb[5:7]

        NS = TOPK * B
        oh_r, sel, oh_t, ecmp = carve(qflat, [NS * P // 2, NS * SEL * NT // 2, NS * NT // 2, NT * E])
        oh_r = oh_r.bitcast(BF16).rearrange("p (n r) -> p n r", n=NS)
        sel = sel.bitcast(BF16).rearrange("p (n g t) -> p n g t", n=NS, g=SEL)
        oh_t = oh_t.bitcast(BF16).rearrange("p (n t) -> p n t", n=NS)
        ecmp = ecmp.rearrange("p (t e) -> p t e", t=NT)

        s_x = [sem(f"x_loaded{i}") for i in range(2)]
        s_c = [sem(f"ctx_loaded{i}") for i in range(2)]
        s_par = sem("params_loaded")
        s_w = sem("experts_loaded")
        s_const = sem("constants_made")
        s_const2 = sem("buffers_cleared")
        s_tg = sem("gains_made")
        s_par2 = sem("params_folded")
        s_rstd0 = sem("var_ready")
        s_xn = sem("xn_ready")
        s_qkt = sem("qk_transposed")
        s_qks = sem("qk_stored")
        s_gate = sem("gates_done")
        s_gsb = sem("gates_stored")
        s_lf = sem("softplus_done")
        s_logf = sem("logf_done")
        s_fps = sem("cumsum_done")
        s_a = sem("a_done")
        s_aT = sem("a_transposed")
        s_mT = sem("mprime_done")
        s_m2 = sem("mprime_transposed")
        s_ml = sem("maxlog_done")
        s_fl = sem("floor_done")
        s_mst = sem("mprime_stored")
        s_bc = [sem(f"mprime_spread{i}") for i in range(3)]
        s_qbd = [sem(f"q_placed{i}") for i in range(2)]
        s_dm = sem("decay_masked")
        s_dec = sem("decay_done")
        s_vp = sem("v_copied")
        s_sc = sem("scores_done")
        s_cm = sem("c_done")
        s_cv = sem("cv_done")
        s_ots = sem("cvT_stored")
        s_ho = sem("cv_transposed")
        s_hn = sem("head_normed")
        s_hs = sem("head_scaled")
        s_x2 = sem("x2_done")
        s_xn2 = sem("xn2_done")
        s_rt = sem("xn2_transposed")
        s_rts = sem("xn2T_stored")
        s_lg = sem("logits_done")
        s_exl = sem("router_exp_done")
        s_mask = sem("mask_done")
        s_rank = sem("ranks_done")
        s_sel = sem("selectors_done")
        s_tab = sem("tables_done")
        s_idx = sem("indices_done")
        s_eti = sem("tile_experts_done")
        s_xno = sem("xn2_written")
        s_x2o = sem("x2_written")
        s_dump = sem("spare_rows_cleared")
        s_xg = [sem(f"tokens_gathered{i}") for i in range(3)]
        s_xt = sem("x_tile_transposed")
        s_xts = sem("x_tile_stored")
        s_gu = sem("gate_up_done")
        s_si = sem("silu_done")
        s_hm = sem("hidden_done")
        s_htp = sem("hidden_transposed")
        s_hts = sem("hiddenT_stored")
        s_y = sem("y_done")
        s_ys = sem("y_scaled")
        s_add = sem("y_added")
        s_vch = sem("vector_step")
        s_sch = sem("scalar_step")
        s_pch = sem("pool_step")

        HB = B // 2
        NPAR = 8
        x_tok = x.rearrange("b s h -> s b h")
        c_tok = ctx_in.rearrange("b s h -> s b h")

        def w_at(name, k, off=0):
            start = {"w1": 0, "w3": KC * I, "w2": 2 * KC * I}[name]
            width = H if name == "w2" else I
            return start + k * width, width

        block = ctx.enter_context(nc.Block())

        @block.sync
        def _(sp):
            for i in range(2):
                sp.dma_start(x_sb[:, i * HB:(i + 1) * HB, :], x_tok[:, i * HB:(i + 1) * HB, :]).then_inc(s_x[i], 16)
                sp.dma_start(ctx_sb[:, i * HB:(i + 1) * HB, :], c_tok[:, i * HB:(i + 1) * HB, :]).then_inc(s_c[i], 16)

            def experts(e):
                for name, w, parts in (("w1", w1, KC), ("w3", w3, KC), ("w2", w2, IC)):
                    at, width = w_at(name, 0)
                    dst = w_sb[:, e * WE + at:e * WE + at + parts * width].rearrange("p (k n) -> p k n", k=parts)
                    sp.dma_start(dst, w[e].rearrange("(k p) n -> p k n", p=P)).then_inc(s_w, 16)

            def place_q(b):
                sp.wait_ge(s_qks, b + 1)
                if b >= 2:
                    sp.wait_ge(s_sc, KC * (b - 1))
                for h in range(HC):
                    rows = slice(h * DH, (h + 1) * DH)
                    sp.dma_start(qbd[rows, b % 2, :, h, :], qkT[rows, b, 0:KC, :]).then_inc(s_qbd[b % 2], 16)

            def spread_m(b):
                if b >= 3:
                    sp.wait_ge(s_cv, KC * (b - 2))
                sp.dma_start(dec[:, b % 3].rearrange("p h s -> p (h s)"),
                             mprime_dram[b:b + 1, :].to_broadcast([P, NH * S])).then_inc(s_bc[b % 3], 16)

            experts(0)
            experts(1)
            sp.wait_ge(s_const2, 2)
            place_q(0)
            place_q(1)
            sp.wait_ge(s_mT, 1)
            sp.dma_start(mprime_dram.rearrange("b (h s) -> (b h) s", s=S), mT[:, :]).then_inc(s_mst, 16)
            sp.wait_ge(s_mst, 16)
            for b in range(3):
                spread_m(b)
            for b in range(B):
                if b + 2 < E:
                    experts(b + 2)
                if b + 2 < B:
                    place_q(b + 2)
                if b + 3 < B:
                    spread_m(b + 3)
                sp.wait_ge(s_xn2, b + 1)
                sp.dma_start(xn_dram[b * S:(b + 1) * S, :], xn_sb[:, b, :]).then_inc(s_xno, 16)
                sp.dma_start(out[b * S:(b + 1) * S, :], x_sb[:, b, :]).then_inc(s_x2o, 16)
            sp.wait_ge(s_add, 16 * NT)

        @block.gpsimd
        def _(pool):
            nc.gpsimd.memset(ident[:], 0.0).then_inc(s_pch, 1)
            nc.gpsimd.memset(tri[:], 1.0).then_inc(s_pch, 1)
            nc.gpsimd.memset(tri_s[:], 1.0).then_inc(s_pch, 1)
            pool.wait_ge(s_pch, 3)
            nc.gpsimd.affine_select(out=ident[:], in_=ident[:], compare_op=ALU.not_equal, fill=1.0, base=0,
                                    pattern=[[-1, P]], channel_multiplier=1).then_inc(s_const, 1)
            nc.gpsimd.affine_select(out=tri[:], in_=tri[:], compare_op=ALU.is_ge, fill=0.0, base=0,
                                    pattern=[[1, P]], channel_multiplier=-1).then_inc(s_const, 1)
            nc.gpsimd.affine_select(out=tri_s[:], in_=tri_s[:], compare_op=ALU.is_gt, fill=0.0, base=0,
                                    pattern=[[1, P]], channel_multiplier=-1).then_inc(s_const, 1)
            nc.gpsimd.memset(vp[:], 0.0).then_inc(s_pch, 1)
            nc.gpsimd.memset(qbd[:], 0.0).then_inc(s_const2, 1)
            nc.gpsimd.memset(ones_b[:], 1.0).then_inc(s_const, 1)
            nc.gpsimd.memset(zrow[:], 0.0).then_inc(s_const, 1)
            nc.gpsimd.memset(zero8[:], 0.0).then_inc(s_const, 1)
            nc.gpsimd.iota(iota_r[:], [[1, P]], base=0, channel_multiplier=0,
                           allow_small_or_imprecise_dtypes=True).then_inc(s_const, 1)
            nc.gpsimd.iota(iota_t[:], [[1, NT]], base=0, channel_multiplier=0,
                           allow_small_or_imprecise_dtypes=True).then_inc(s_const, 1)
            nc.gpsimd.iota(iota_c[:], [[P, E]], base=0, channel_multiplier=0,
                           allow_small_or_imprecise_dtypes=True).then_inc(s_const, 1)
            nc.gpsimd.iota(iota_e[:], [[-1, E]], base=E, channel_multiplier=0,
                           allow_small_or_imprecise_dtypes=True).then_inc(s_const, 1)
            nc.gpsimd.iota(tok_p[:], [[0, 1]], base=0, channel_multiplier=1,
                           allow_small_or_imprecise_dtypes=True).then_inc(s_const, 1)
            nc.gpsimd.iota(tok_j[:], [[S, B]], base=0, channel_multiplier=0,
                           allow_small_or_imprecise_dtypes=True).then_inc(s_const, 1)
            nc.gpsimd.iota(dump[:], [[0, 1]], base=T, channel_multiplier=1,
                           allow_small_or_imprecise_dtypes=True).then_inc(s_const, 1)
            pool.wait_ge(s_pch, 4)
            nc.gpsimd.memset(vp[:, :, :, DH:DH + 1], 1.0).then_inc(s_const2, 1)
            pool.wait_ge(s_const, 13)
            pool.dma_start(out[T:T + P, :], zrow[:, :]).then_inc(s_dump, 16)

            for b in range(B + 1):
                if b < B:
                    pool.wait_ge(s_bc[b % 3], 16 * (b // 3 + 1))
                    for c in range(KC):
                        v = dec[:, b % 3, c * HC:(c + 1) * HC, :]
                        nc.gpsimd.affine_select(out=v, in_=v, compare_op=ALU.is_ge, fill=BIG, base=0,
                                                pattern=[[0, HC], [1, S]], channel_multiplier=-1).then_inc(s_dm, 1)
                if b >= 1:
                    pool.wait_ge(s_hn, b)
                    pool.wait_ge(s_par2, 2)
                    hv = hh.rearrange("p h d -> p (h d)")
                    nc.gpsimd.tensor_tensor(hq.rearrange("p h d -> p (h d)"), hv, lns[:], ALU.mult).then_inc(s_hs, 1)
                    pool.wait_ge(s_hs, b)
                    nc.gpsimd.tensor_tensor(x_sb[:, b - 1, :], x_sb[:, b - 1, :],
                                            hq.rearrange("p h d -> p (h d)"), ALU.add).then_inc(s_x2, 1)

            def gather(i):
                if i >= 3:
                    pool.wait_ge(s_xt, i - 2)
                nc.gpsimd.indirect_dma_start(
                    out=xg_sb[i % 3], out_offset=None, in_=xn_dram[:, :],
                    in_offset=bass.IndirectOffsetOnAxis(ap=gidx[:, i:i + 1], axis=0)).then_inc(s_xg[i % 3], 16)

            pool.wait_ge(s_idx, 1)
            pool.wait_ge(s_xno, 16 * B)
            for i in range(3):
                gather(i)
            pool.wait_ge(s_x2o, 16 * B)
            pool.wait_ge(s_dump, 16)
            for i in range(NT):
                pool.wait_ge(s_ys, i + 1)
                if i >= 1:
                    pool.wait_ge(s_add, 16 * i)
                nc.gpsimd.indirect_dma_start(
                    out=out[:, :], out_offset=bass.IndirectOffsetOnAxis(ap=sidx[:, i:i + 1], axis=0),
                    in_=y_sb[i % 2], in_offset=None, compute_op=ALU.add).then_inc(s_add, 16)
                if i + 3 < NT:
                    gather(i + 3)
            pool.wait_ge(s_add, 16 * NT)

        @block.scalar
        def _(act):
            act.dma_start(gx[:, 0:1], g_xattn.rearrange("(a b) -> a b", a=1).to_broadcast([P, 1])).then_inc(s_par, 16)
            act.dma_start(gx[:, 1:2], g_ffn.rearrange("(a b) -> a b", a=1).to_broadcast([P, 1])).then_inc(s_par, 16)
            act.dma_start(wg_sb[:, :, 0:NH], wi.rearrange("(c p) h -> p c h", p=P)).then_inc(s_par, 16)
            act.dma_start(wg_sb[:, :, NH:G2], wf.rearrange("(c p) h -> p c h", p=P)).then_inc(s_par, 16)
            act.dma_start(gb_sb[:, 0:NH], bi.rearrange("(a h) -> a h", a=1).to_broadcast([P, NH])).then_inc(s_par, 16)
            act.dma_start(gb_sb[:, NH:G2], bf.rearrange("(a h) -> a h", a=1).to_broadcast([P, NH])).then_inc(s_par, 16)
            act.dma_start(lns[:], ln_scale.rearrange("(a h) -> a h", a=1).to_broadcast([P, H])).then_inc(s_par, 16)
            act.dma_start(wr_sb[:], w_gate.rearrange("(c p) e -> p c e", p=P)).then_inc(s_par, 16)
            act.wait_ge(s_par, 16 * NPAR)
            nc.scalar.activation(tg[:], gx[:], ACT.Tanh).then_inc(s_tg, 1)

            for b in range(B):
                act.wait_ge(s_qkt, b + 1)
                nc.scalar.activation(qkT[:, b].rearrange("p c s -> p (c s)"), (ps_tr if b % 2 == 0 else ps_h)[:, :],
                                     ACT.Copy).then_inc(s_qks, 1)
            f_all = gates[:, :, 1, :]
            v3 = lambda t: t.rearrange("p (b h) -> p b h", b=B)
            act.wait_ge(s_gsb, 1)
            nc.scalar.activation(v3(fa[:]), f_all, ACT.Abs).then_inc(s_sch, 1)
            act.wait_ge(s_sch, 1)
            nc.scalar.activation(fu[:], fa[:], ACT.Exp, scale=-1.0).then_inc(s_sch, 1)
            act.wait_ge(s_sch, 2)
            act.wait_ge(s_const2, 3)
            nc.scalar.activation(fl[:], fu[:], ACT.Ln, bias=one_c[:, 0:1]).then_inc(s_lf, 1)
            act.wait_ge(s_ml, 1)
            nc.scalar.activation(floor[:], mlog[:], ACT.Exp, scale=-1.0).then_inc(s_fl, 1)

            def copy_v(b):
                if b >= 2:
                    act.wait_ge(s_cv, KC * (b - 1))
                nc.scalar.activation(vp[:, b % 2, :, 0:DH], ctx_sb[:, b].rearrange("p (h d) -> p h d", h=NH),
                                     ACT.Copy).then_inc(s_vp, 1)

            def decay(b, c):
                act.wait_ge(s_dm, KC * b + c + 1)
                for h in range(c * HC, (c + 1) * HC):
                    d = dec[:, b % 3, h, :]
                    last = nc.scalar.activation(d, d, ACT.Exp, bias=amat[:, b * NH + h:b * NH + h + 1], scale=-1.0)
                last.then_inc(s_dec, 1)

            act.wait_ge(s_const2, 2)
            act.wait_ge(s_c[0], 16)
            act.wait_ge(s_c[1], 16)
            act.wait_ge(s_a, 1)
            copy_v(0)
            decay(0, 0)
            decay(0, 1)
            for b in range(B + 2):
                if b + 1 < B:
                    copy_v(b + 1)
                    decay(b + 1, 0)
                if b >= 2:
                    act.wait_ge(s_rt, b - 1)
                    if b >= 3:
                        act.wait_ge(s_lg, b - 2)
                    nc.scalar.activation(xlT[:], ps_tr[:, 0:H], ACT.Copy).then_inc(s_rts, 1)
                if b < B:
                    act.wait_ge(s_cv, KC * (b + 1))
                    if b >= 1:
                        act.wait_ge(s_ho, b)
                    nc.scalar.activation(cvT[:], ps_ht[:, :], ACT.Copy).then_inc(s_ots, 1)
                if b + 1 < B:
                    decay(b + 1, 1)

            act.wait_ge(s_lg, B)
            nc.scalar.activation(lt.rearrange("p b e -> p (b e)"), ps_small[:, 0:B * E], ACT.Tanh,
                                 scale=1.0 / SOFTCAP).then_inc(s_sch, 1)
            act.wait_ge(s_sch, 3)
            nc.scalar.activation(ex[:], lt[:], ACT.Exp, scale=SOFTCAP).then_inc(s_exl, 1)

            def silu(i, p):
                act.wait_ge(s_gu, i + 1)
                nc.scalar.activation(sg_sb[p], ps_scores[p][:, 0, :], ACT.Silu).then_inc(s_si, 1)

            def store_hT(i, p):
                act.wait_ge(s_htp, i + 1)
                nc.scalar.activation(hT_sb[p], ps_ht[:, :], ACT.Copy).then_inc(s_hts, 1)

            silu(0, 0)
            with act.Fori(0, NT - 1, 2) as i:
                store_hT(i, 0)
                silu(i + 1, 1)
                store_hT(i + 1, 1)
                silu(i + 2, 0)
            store_hT(NT - 1, 0)

        @block.vector
        def _(dve):
            chain = [0]

            def link(ins):
                chain[0] += 1
                ins.then_inc(s_vch, 1)
                dve.wait_ge(s_vch, chain[0])

            def rsqrt(y, v, t):
                yi, vi = y.bitcast(I32), v.bitcast(I32)
                link(nc.vector.tensor_scalar(yi, vi, 1, None, ALU.logical_shift_right))
                link(nc.vector.tensor_scalar(yi, yi, -1.0, float(RSQRT_MAGIC), ALU.mult, ALU.add))
                for _ in range(3):
                    link(nc.vector.tensor_tensor(t, y, y, ALU.mult))
                    link(nc.vector.scalar_tensor_tensor(out=t, in0=t, scalar=-0.5, in1=v, op0=ALU.mult, op1=ALU.mult))
                    link(nc.vector.scalar_tensor_tensor(out=y, in0=t, scalar=1.5, in1=y, op0=ALU.add, op1=ALU.mult))

            nc.vector.memset(one_c[:], 1.0).then_inc(s_const2, 1)
            for i in range(2):
                dve.wait_ge(s_x[i], 16)
                for b in range(i * HB, (i + 1) * HB):
                    nc.vector.bn_stats(st[:, b, :], x_sb[:, b, :]).then_inc(s_vch, 1)
                    chain[0] += 1
                dve.wait_ge(s_vch, chain[0])
                for b in range(i * HB, (i + 1) * HB):
                    nc.vector.bn_aggr(mv[:, b, :], st[:, b, :]).then_inc(s_vch, 1)
                    chain[0] += 1
                dve.wait_ge(s_vch, chain[0])
                hb = slice(i * HB, (i + 1) * HB)
                link(nc.vector.tensor_scalar(rs[:, 0, 0:HB], mv[:, hb, 1], LN_EPS, None, ALU.add))
                rsqrt(rs[:, 1, 0:HB], rs[:, 0, 0:HB], rs[:, 2, 0:HB])
                for b in range(i * HB, (i + 1) * HB):
                    k = b - i * HB
                    nc.vector.tensor_scalar(xn_sb[:, b, :], x_sb[:, b, :], mv[:, b, 0:1], rs[:, 1, k:k + 1],
                                            ALU.subtract, ALU.mult).then_inc(s_xn, 1)
                if i == 0:
                    dve.wait_ge(s_par, 16 * NPAR)
                    nc.vector.tensor_tensor(wg_sb[:, KC:2 * KC, :], wg_sb[:, KC:2 * KC, :], wg_sb[:, 2 * KC:3 * KC, :],
                                            ALU.add).then_inc(s_par2, 1)
                    dve.wait_ge(s_tg, 1)
                    nc.vector.tensor_scalar(lns[:], lns[:], tg[:, 0:1], None, ALU.mult).then_inc(s_par2, 1)

            dve.wait_ge(s_gate, B)
            nc.vector.tensor_tensor(gates.rearrange("p b g h -> p b (g h)"),
                                    ps_small[:, 0:B * G2].rearrange("p (b g) -> p b g", b=B),
                                    gb_sb[:, :].unsqueeze(1).to_broadcast([P, B, G2]), ALU.add).then_inc(s_gsb, 1)
            dve.wait_ge(s_lf, 1)
            v3 = lambda t: t.rearrange("p (b h) -> p b h", b=B)
            nc.vector.scalar_tensor_tensor(out=v3(logf[:]), in0=gates[:, :, 1, :], scalar=0.0, in1=v3(fl[:]),
                                           op0=ALU.min, op1=ALU.subtract).then_inc(s_logf, 1)
            dve.wait_ge(s_fps, 1)
            link(nc.vector.tensor_copy(fcum[:], ps_ht[:, 0:BH]))
            nc.vector.tensor_tensor(v3(amat[:]), gates[:, :, 0, :], v3(fcum[:]), ALU.subtract).then_inc(s_a, 1)
            dve.wait_ge(s_aT, 1)
            link(nc.vector.tensor_copy(aT[:], ps_ht[:, BH:2 * BH]))
            nc.vector.tensor_tensor_scan(mT[:], aT[:], aT[:], -3.0e38, ALU.max, ALU.max).then_inc(s_mT, 1)
            dve.wait_ge(s_m2, 1)
            nc.vector.tensor_tensor(mlog[:], ps_ht[:, 2 * BH:3 * BH], fcum[:], ALU.add).then_inc(s_ml, 1)

            def c_mult(b, c):
                dve.wait_ge(s_sc, KC * b + c + 1)
                dve.wait_ge(s_dec, KC * b + c + 1)
                d = dec[:, b % 3, c * HC:(c + 1) * HC, :].rearrange("p h s -> p (h s)")
                nc.vector.scalar_tensor_tensor(out=d, in0=ps_scores[c].rearrange("p a n -> p (a n)"),
                                               scalar=float(DH) ** -0.5, in1=d,
                                               op0=ALU.mult, op1=ALU.mult).then_inc(s_cm, 1)

            def per_head(t):
                return t.unsqueeze(2).to_broadcast([P, NH, DH])

            def norm_heads(b):
                dve.wait_ge(s_ho, b + 1)
                cv = ps_h.rearrange("p (h v) -> p h v", v=VW)
                if b == 0:
                    dve.wait_ge(s_fl, 1)
                link(nc.vector.tensor_scalar(s16[:, 5, :], cv[:, :, DH], -1.0, None, ALU.mult))
                link(nc.vector.tensor_tensor(s16[:, 5, :], s16[:, 5, :], cv[:, :, DH], ALU.max))
                link(nc.vector.tensor_tensor(s16[:, 0, :], s16[:, 5, :], floor[:, b * NH:(b + 1) * NH], ALU.max))
                link(nc.vector.tensor_scalar(s16[:, 1, :], s16[:, 0, :], MLSTM_EPS, None, ALU.add))
                link(nc.vector.reciprocal(s16[:, 2, :], s16[:, 1, :]))
                link(nc.vector.tensor_tensor(hc[:], cv[:, :, 0:DH], per_head(s16[:, 2, :]), ALU.mult))
                link(nc.vector.tensor_reduce(s16[:, 3, :], hc[:], AX_X, ALU.add))
                link(nc.vector.tensor_scalar(s16[:, 3, :], s16[:, 3, :], 1.0 / DH, None, ALU.mult))
                if b >= 1:
                    dve.wait_ge(s_hs, b)
                link(nc.vector.tensor_tensor(hc[:], hc[:], per_head(s16[:, 3, :]), ALU.subtract))
                link(nc.vector.tensor_tensor(hh[:], hc[:], hc[:], ALU.mult))
                link(nc.vector.tensor_reduce(s16[:, 4, :], hh[:], AX_X, ALU.add))
                link(nc.vector.tensor_scalar(rs[:, 0, :], s16[:, 4, :], 1.0 / DH, MLSTM_EPS, ALU.mult, ALU.add))
                rsqrt(rs[:, 1, :], rs[:, 0, :], rs[:, 2, :])
                nc.vector.tensor_tensor(hh[:], hc[:], per_head(rs[:, 1, :]), ALU.mult).then_inc(s_hn, 1)

            def norm_x2(b):
                dve.wait_ge(s_x2, b + 1)
                link(nc.vector.bn_stats(st[:, b, :], x_sb[:, b, :]))
                link(nc.vector.bn_aggr(mv[:, b, :], st[:, b, :]))
                link(nc.vector.tensor_scalar(rs[:, 0, 0:1], mv[:, b, 1:2], LN_EPS, None, ALU.add))
                rsqrt(rs[:, 1, 0:1], rs[:, 0, 0:1], rs[:, 2, 0:1])
                nc.vector.tensor_scalar(xn_sb[:, b, :], x_sb[:, b, :], mv[:, b, 0:1], rs[:, 1, 0:1],
                                        ALU.subtract, ALU.mult).then_inc(s_xn2, 1)

            for b in range(B + 1):
                if b < B:
                    c_mult(b, 0)
                    c_mult(b, 1)
                if b >= 2:
                    norm_x2(b - 2)
                if b >= 1:
                    norm_heads(b - 1)
            norm_x2(B - 1)

            be = lambda t: t.unsqueeze(2).to_broadcast([P, B, E])
            rev = iota_e[:, :].unsqueeze(1).to_broadcast([P, B, E])
            dve.wait_ge(s_const, 13)
            dve.wait_ge(s_exl, 1)
            src = ex
            for k in range(TOPK):
                link(nc.vector.tensor_reduce(r8[:, k, :], src[:], AX_X, ALU.max))
                link(nc.vector.tensor_tensor(key[:], src[:], be(r8[:, k, :]), ALU.is_equal))
                link(nc.vector.tensor_tensor(key[:], key[:], rev, ALU.mult))
                link(nc.vector.tensor_reduce(r8[:, 2, :], key[:], AX_X, ALU.max))
                link(nc.vector.tensor_tensor(oh[:, k], key[:], be(r8[:, 2, :]), ALU.is_equal))
                if k == 0:
                    link(nc.vector.scalar_tensor_tensor(out=ex2[:], in0=oh[:, 0], scalar=-BIG, in1=ex[:],
                                                        op0=ALU.mult, op1=ALU.add))
                    src = ex2
            nc.vector.tensor_tensor(mask[:], oh[:, 0], oh[:, 1], ALU.add).then_inc(s_mask, 1)
            link(nc.vector.tensor_reduce(r8[:, 3, :], ex[:], AX_X, ALU.add))
            link(nc.vector.reciprocal(r8[:, 4, :], r8[:, 3, :]))
            link(nc.vector.tensor_scalar(r8[:, 4, :], r8[:, 4, :], tg[:, 1:2], None, ALU.mult))
            link(nc.vector.tensor_tensor(wsel[:], r8[:, 0:TOPK, :],
                                         r8[:, 4, :].unsqueeze(1).to_broadcast([P, TOPK, B]), ALU.mult))
            wf = wsel.rearrange("p k b -> p (k b)")
            link(nc.vector.tensor_copy(wpart[:, 0, :], wf))
            link(nc.vector.tensor_tensor(wres[:, 0, :], wf, wpart[:, 0, :], ALU.subtract))
            link(nc.vector.tensor_copy(wpart[:, 1, :], wres[:, 0, :]))
            link(nc.vector.tensor_tensor(wres[:, 1, :], wres[:, 0, :], wpart[:, 1, :], ALU.subtract))
            link(nc.vector.tensor_copy(wpart[:, 2, :], wres[:, 1, :]))

            dve.wait_ge(s_rank, 1)
            link(nc.vector.tensor_copy(cnt[:], ps_small[:, 192:192 + E]))
            link(nc.vector.tensor_tensor(ctile[:], cnt[:, :].unsqueeze(2).to_broadcast([P, E, E]),
                                         iota_c[:, :].unsqueeze(1).to_broadcast([P, E, E]), ALU.is_gt))
            link(nc.vector.tensor_reduce(ntile[:], ctile[:], AX_X, ALU.add))
            link(nc.vector.tensor_tensor_scan(etile[:], ntile[:], zero8[:], 0.0, ALU.add, ALU.add))
            link(nc.vector.tensor_tensor(base[:], etile[:], ntile[:], ALU.subtract))
            link(nc.vector.tensor_scalar(base[:], base[:], float(P), None, ALU.mult))
            link(nc.vector.tensor_tensor(slotm[:], ps_small[:, 128:128 + B * E].rearrange("p (b e) -> p b e", b=B),
                                         base[:, :].unsqueeze(1).to_broadcast([P, B, E]), ALU.add))
            for k in range(TOPK):
                link(nc.vector.tensor_tensor(slotk[:, k], oh[:, k], slotm[:], ALU.mult))
            link(nc.vector.tensor_reduce(slotf[:], slotk.rearrange("p k b e -> p (k b) e"), AX_X, ALU.add))
            link(nc.vector.tensor_copy(sloti[:, 0, :], slotf[:]))
            link(nc.vector.tensor_scalar(sloti[:, 1, :], sloti[:, 0, :], P - 1, None, ALU.bitwise_and))
            link(nc.vector.tensor_scalar(sloti[:, 2, :], sloti[:, 0, :], 7, None, ALU.logical_shift_right))
            link(nc.vector.tensor_copy(srf[:], sloti[:, 1:3, :]))
            link(nc.vector.tensor_tensor(oh_t[:], iota_t[:, :].unsqueeze(1).to_broadcast([P, NS, NT]),
                                         srf[:, 1, :].unsqueeze(2).to_broadcast([P, NS, NT]), ALU.is_equal))
            tj = tok_j[:, :].unsqueeze(1).to_broadcast([P, TOPK, B])
            link(nc.vector.tensor_copy(wres[:, 0, :].rearrange("p (k b) -> p k b", k=TOPK), tj))
            nt = lambda t: t.unsqueeze(2).to_broadcast([P, NS, NT])
            link(nc.vector.tensor_scalar(sel[:, :, 0, :], oh_t[:], tok_p[:, 0:1], None, ALU.mult))
            link(nc.vector.tensor_tensor(sel[:, :, 1, :], oh_t[:], nt(wres[:, 0, :]), ALU.mult))
            link(nc.vector.tensor_copy(sel[:, :, 2, :], oh_t[:]))
            for j in range(3):
                link(nc.vector.tensor_tensor(sel[:, :, 3 + j, :], oh_t[:], nt(wpart[:, j, :]), ALU.mult))
            nc.vector.tensor_tensor(oh_r[:], iota_r[:, :].unsqueeze(1).to_broadcast([P, NS, P]),
                                    srf[:, 0, :].unsqueeze(2).to_broadcast([P, NS, P]),
                                    ALU.is_equal).then_inc(s_sel, 1)
            link(nc.vector.tensor_tensor(ecmp[:], iota_t[:, :].unsqueeze(2).to_broadcast([P, NT, E]),
                                         etile[:, :].unsqueeze(1).to_broadcast([P, NT, E]), ALU.is_ge))
            link(nc.vector.tensor_reduce(etf[:], ecmp[:], AX_X, ALU.add))
            nc.vector.tensor_scalar(eti[:], etf[:], float(E - 1), None, ALU.min).then_inc(s_eti, 1)

            dve.wait_ge(s_tab, 1)
            link(nc.vector.tensor_copy(tab.rearrange("p g t -> p (g t)"), ps_small[:, 256:256 + SEL * NT]))
            link(nc.vector.tensor_tensor(tokf[:, 0, :], tab[:, 0, :], tab[:, 1, :], ALU.add))
            link(nc.vector.tensor_copy(gidx[:], tokf[:, 0, :]))
            link(nc.vector.tensor_scalar(tokf[:, 1, :], tab[:, 2, :], -1.0, 1.0, ALU.mult, ALU.add))
            link(nc.vector.scalar_tensor_tensor(out=tokf[:, 1, :], in0=tokf[:, 1, :], scalar=dump[:, 0:1],
                                                in1=tokf[:, 0, :], op0=ALU.mult, op1=ALU.add))
            nc.vector.tensor_copy(sidx[:], tokf[:, 1, :]).then_inc(s_idx, 1)
            link(nc.vector.tensor_tensor(wslot[:, 0:NT], tab[:, 3, :], tab[:, 4, :], ALU.add))
            link(nc.vector.tensor_tensor(wslot[:, 0:NT], wslot[:, 0:NT], tab[:, 5, :], ALU.add))

            def store_xT(i, p):
                dve.wait_ge(s_xt, i + 1)
                nc.vector.tensor_copy(xT_sb[p], ps_h[:, 0:H]).then_inc(s_xts, 1)

            def hidden(i, p):
                dve.wait_ge(s_si, i + 1)
                nc.vector.tensor_tensor(h_sb[p], sg_sb[p], ps_scores[p][:, 1, :], ALU.mult).then_inc(s_hm, 1)

            def scale_y(i, p, first=False):
                dve.wait_ge(s_y, i + 1)
                if not first:
                    dve.wait_ge(s_add, 16 * i - 16)
                nc.vector.tensor_scalar(y_sb[p], ps_tr[:, 0:H], wslot[:, bass.ds(i, 1)], None,
                                        ALU.mult).then_inc(s_ys, 1)

            store_xT(0, 0)
            store_xT(1, 1)
            hidden(0, 0)
            store_xT(2, 0)
            hidden(1, 1)
            scale_y(0, 0, True)
            store_xT(3, 1)
            hidden(2, 0)
            scale_y(1, 1, True)
            with dve.Fori(2, NT - 3, 2) as i:
                store_xT(i + 2, 0)
                hidden(i + 1, 1)
                scale_y(i, 0)
                store_xT(i + 3, 1)
                hidden(i + 2, 0)
                scale_y(i + 1, 1)
            store_xT(NT - 1, 0)
            hidden(NT - 2, 1)
            scale_y(NT - 3, 0)
            hidden(NT - 1, 0)
            scale_y(NT - 2, 1)
            scale_y(NT - 1, 0)

        @block.tensor
        def _(pe):
            pe.wait_ge(s_const, 13)
            for b in range(B + 1):
                if b < B:
                    pe.wait_ge(s_xn, b + 1)
                    pe.wait_ge(s_c[b // HB], 16)
                    if b >= 2:
                        pe.wait_ge(s_qks, b - 1)
                    bk = ps_tr if b % 2 == 0 else ps_h
                    for c in range(KC):
                        nc.tensor.transpose(bk[:, c * P:(c + 1) * P], xn_sb[:, b, c * P:(c + 1) * P], ident[:])
                    for c in range(KC):
                        last = nc.tensor.transpose(bk[:, (KC + c) * P:(KC + c + 1) * P],
                                                   ctx_sb[:, b, c * P:(c + 1) * P], ident[:])
                    last.then_inc(s_qkt, 1)
                if b >= 1:
                    pe.wait_ge(s_qks, b)
                    if b == 1:
                        pe.wait_ge(s_par2, 1)
                    for c in range(2 * KC):
                        last = nc.tensor.matmul(ps_small[:, (b - 1) * G2:b * G2], qkT[:, b - 1, c, :], wg_sb[:, c, :],
                                                start=(c == 0), stop=(c == 2 * KC - 1))
                    last.then_inc(s_gate, 1)
            pe.wait_ge(s_logf, 1)
            nc.tensor.matmul(ps_ht[:, 0:BH], tri[:], logf[:], start=True, stop=True).then_inc(s_fps, 1)
            pe.wait_ge(s_a, 1)
            nc.tensor.transpose(ps_ht[:, BH:2 * BH], amat[:], ident[:]).then_inc(s_aT, 1)
            pe.wait_ge(s_mT, 1)
            nc.tensor.transpose(ps_ht[:, 2 * BH:3 * BH], mT[:], ident[:]).then_inc(s_m2, 1)

            def scores(b, c):
                if c == 0:
                    pe.wait_ge(s_qbd[b % 2], 16 * HC * (b // 2 + 1))
                if b >= 1:
                    pe.wait_ge(s_cm, KC * (b - 1) + c + 1)
                for half in range(2):
                    rhs = qbd[:, b % 2, c, half * 4:(half + 1) * 4, :].rearrange("p h s -> p (h s)")
                    last = nc.tensor.matmul(ps_scores[c][:, half, :], qkT[:, b, KC + c, :], rhs, start=True, stop=True)
                last.then_inc(s_sc, 1)

            def cv(b, c):
                pe.wait_ge(s_cm, KC * b + c + 1)
                if c == 0:
                    pe.wait_ge(s_vp, b + 1)
                    if b >= 1:
                        pe.wait_ge(s_ots, b)
                    else:
                        pe.wait_ge(s_ml, 1)
                for h in range(c * HC, (c + 1) * HC):
                    g, j = h // 4, h % 4
                    last = nc.tensor.matmul(ps_ht[j * VW:(j + 1) * VW, g * P:(g + 1) * P], vp[:, b % 2, h, :],
                                            dec[:, b % 3, h, :], start=True, stop=True, tile_position=(0, j * VW))
                last.then_inc(s_cv, 1)

            def turn_cv(b):
                pe.wait_ge(s_ots, b + 1)
                if b >= 1:
                    pe.wait_ge(s_hn, b)
                for g in range(4):
                    last = nc.tensor.transpose(ps_h[:, g * P:(g + 1) * P], cvT[:, g * P:(g + 1) * P], ident[:])
                last.then_inc(s_ho, 1)

            def turn_x2(b):
                pe.wait_ge(s_xn2, b + 1)
                if b >= 1:
                    pe.wait_ge(s_rts, b)
                for c in range(KC):
                    last = nc.tensor.transpose(ps_tr[:, c * P:(c + 1) * P], xn_sb[:, b, c * P:(c + 1) * P], ident[:])
                last.then_inc(s_rt, 1)

            def logits(b):
                pe.wait_ge(s_rts, b + 1)
                for c in range(KC):
                    last = nc.tensor.matmul(ps_small[:, b * E:(b + 1) * E], xlT[:, c * P:(c + 1) * P], wr_sb[:, c, :],
                                            start=(c == 0), stop=(c == KC - 1))
                last.then_inc(s_lg, 1)

            for b in range(B + 3):
                if b < B:
                    scores(b, 0)
                if b >= 3:
                    logits(b - 3)
                if 1 <= b <= B:
                    turn_cv(b - 1)
                if b < B:
                    scores(b, 1)
                    cv(b, 0)
                    cv(b, 1)
                if 2 <= b < B + 2:
                    turn_x2(b - 2)

            pe.wait_ge(s_mask, 1)
            NR = B * E
            rank = ps_small[:, 128:128 + NR]
            mk = mask.rearrange("p b e -> p (b e)")
            nc.tensor.matmul(rank, tri_s[:], mk, start=True, stop=True)
            for i in range(B - 1):
                nc.tensor.matmul(rank[:, (i + 1) * E:], ones_b[:],
                                 mask[:, i:i + 1, :].to_broadcast([P, B - 1 - i, E]),
                                 start=False, stop=True, skip_group_check=True)
            for i in range(B):
                last = nc.tensor.matmul(ps_small[:, 192:192 + E], ones_b[:], mk[:, i * E:(i + 1) * E],
                                        start=(i == 0), stop=(i == B - 1), skip_group_check=True)
            last.then_inc(s_rank, 1)
            pe.wait_ge(s_sel, 1)
            for n in range(TOPK * B):
                last = nc.tensor.matmul(ps_small[:, 256:256 + SEL * NT], oh_r[:, n, :],
                                        sel[:, n].rearrange("p g t -> p (g t)"),
                                        start=(n == 0), stop=(n == TOPK * B - 1))
            last.then_inc(s_tab, 1)

            def turn_x(i, slot_sem, n, p3, xts=None):
                pe.wait_ge(slot_sem, n)
                if xts is not None:
                    pe.wait_ge(s_xts, xts)
                for c in range(KC):
                    last = nc.tensor.transpose(ps_h[:, c * P:(c + 1) * P], xg_sb[p3][:, c * P:(c + 1) * P], ident[:])
                last.then_inc(s_xt, 1)

            def expert_of(i):
                return pe.value_load(eti[0:1, bass.ds(i, 1)], min_val=0, max_val=E - 1)

            def gate_up(i, p, e):
                pe.wait_ge(s_xts, i + 1)
                for n, name in enumerate(("w1", "w3")):
                    for k in range(KC):
                        at, width = w_at(name, k)
                        last = nc.tensor.matmul(ps_scores[p][:, n, :], xT_sb[p][:, k * P:(k + 1) * P],
                                                w_sb[:, bass.ds(e * WE + at, width)],
                                                start=(k == 0), stop=(k == KC - 1))
                last.then_inc(s_gu, 1)

            def turn_h(i, p, hts=True):
                pe.wait_ge(s_hm, i + 1)
                if hts:
                    pe.wait_ge(s_hts, i)
                for c in range(IC):
                    last = nc.tensor.transpose(ps_ht[:, c * P:(c + 1) * P], h_sb[p][:, c * P:(c + 1) * P], ident[:])
                last.then_inc(s_htp, 1)

            def down(i, p, e, ys=True):
                pe.wait_ge(s_hts, i + 1)
                if ys:
                    pe.wait_ge(s_ys, i)
                for k in range(IC):
                    at, width = w_at("w2", k)
                    last = nc.tensor.matmul(ps_tr[:, 0:H], hT_sb[p][:, k * P:(k + 1) * P],
                                            w_sb[:, bass.ds(e * WE + at, width)],
                                            start=(k == 0), stop=(k == IC - 1))
                last.then_inc(s_y, 1)

            pe.wait_ge(s_w, 16 * 3 * E)
            pe.wait_ge(s_eti, 1)
            for i in range(NT + 1):
                if i == 0:
                    turn_x(0, s_xg[0], 16, 0)
                if i >= 1:
                    turn_h(i - 1, (i - 1) % 2, i >= 2)
                if i < NT:
                    gate_up(i, i % 2, expert_of(i))
                if i + 1 < NT:
                    turn_x(i + 1, s_xg[(i + 1) % 3], 16 * ((i + 1) // 3 + 1), (i + 1) % 3, i + 1)
                if i >= 1:
                    down(i - 1, (i - 1) % 2, expert_of(i - 1), i >= 2)


_INS = ['x', 'ctx_2048', 'g_xattn', 'g_ffn', 'L0_xattn_Wi', 'L0_xattn_bi', 'L0_xattn_Wf', 'L0_xattn_bf',
        'L0_xattn_ln_scale', 'L0_ffn_w_gate', 'L0_ffn_w1', 'L0_ffn_w3', 'L0_ffn_w2']


def kernel(**inputs):
    import numpy as _np
    import concourse.bacc as _bacc
    from concourse import mybir as _mybir
    from concourse.bass_utils import run_bass_kernel_spmd as _run

    nc = _bacc.Bacc("TRN2", target_bir_lowering=False, num_devices=1)
    arrays, args = {}, []
    for name in _INS:
        a = _np.ascontiguousarray(inputs[name])
        arrays[f"in_{name}_dram"] = a
        args.append(nc.dram_tensor(f"in_{name}_dram", a.shape, _mybir.dt.from_np(a.dtype), kind="ExternalInput").ap())
    b, s, h = inputs['x'].shape
    args.append(nc.dram_tensor("out_0_dram", (b * s + 128, h), F32, kind="ExternalOutput").ap())
    bass_gated_mlstm_moe_kernel(nc, *args)
    r = _run(nc, [arrays], core_ids=[0])
    return r.results[0]["out_0_dram"][:b * s].reshape(b, s, h)
```

```python
from contextlib import ExitStack

import concourse.bass as bass
from concourse import mybir

F32 = mybir.dt.float32
BF16 = mybir.dt.bfloat16
I32 = mybir.dt.int32
ALU = mybir.AluOpType
ACT = mybir.ActivationFunctionType
AX_X = mybir.AxisListType.X

P = 128
BIG = 1.0e30
LN_EPS = 1e-5
MLSTM_EPS = 1e-6
SOFTCAP = 30.0
RSQRT_MAGIC = 0x5F3759DF


def bass_gated_mlstm_moe_kernel(nc, x, ctx_in, g_xattn, g_ffn, wi, bi, wf, bf, ln_scale, w_gate, w1, w3, w2, out):
    B, S, H = x.shape
    NH = wi.shape[1]
    DH = H // NH
    KC = H // P
    E = w_gate.shape[1]
    I = w1.shape[2]
    IC = I // P
    T = B * S
    TOPK = 2
    HC = NH // KC
    VW = 32
    NT = TOPK * T // P + E - 1
    assert S == P and NT % 2 == 1 and (NT - 1) * P <= TOPK * T + E * (P - 1) < (NT + 1) * P
    G2 = 2 * NH
    BH = B * NH
    SEL = 6
    WE = 2 * KC * I + IC * H

    mprime_dram = nc.dram_tensor("mprime_scratch", [B, NH * S], F32, kind="Internal").ap()
    xn_dram = nc.dram_tensor("xnorm_scratch", [T, H], F32, kind="Internal").ap()

    with ExitStack() as ctx:
        def sb(name, shape, dt=F32):
            return ctx.enter_context(nc.sbuf_tensor(name, shape, dt))

        def sem(name):
            return ctx.enter_context(nc.semaphore(name))

        bank = [ctx.enter_context(nc.psum_tensor(f"bank{i}", [P, 2, 512] if i < 2 else [P, 512], F32)) for i in range(6)]
        ps_scores = bank[0:2]
        ps_ht = bank[2]
        ps_h = bank[3]
        ps_tr = bank[4]
        ps_small = bank[5]

        w_sb = sb("w_sb", [P, E * WE])
        x_sb = sb("x_sb", [P, B, H])
        ctx_sb = sb("ctx_sb", [P, B, H])
        xn_sb = sb("xn_sb", [P, B, H])
        qkT = sb("qkT", [P, B, 2 * KC, S])
        qbd = sb("qbd", [P, 2, KC, HC, S])
        dec = sb("dec", [P, 3, NH, S])
        vp = sb("vp", [P, 2, NH, VW])
        wg_sb = sb("wg_sb", [P, 3 * KC, G2])
        gb_sb = sb("gb_sb", [G2, 1])
        gT_sb = sb("gT_sb", [G2, B // 2, S])
        wr_sb = sb("wr_sb", [P, KC, E])
        lns = sb("lns", [P, H])
        gx = sb("gx", [P, 2])
        tg = sb("tg", [P, 2])
        ident = sb("ident", [P, P])
        tri = sb("tri", [P, P])
        rstd2 = sb("rstd2", [P, B])
        tri_s = sb("tri_s", [P, P], BF16)
        ones_b = sb("ones_b", [P, P], BF16)
        iota_r = sb("iota_r", [P, P])
        iota_t = sb("iota_t", [P, NT])
        iota_c = sb("iota_c", [P, E])
        iota_e = sb("iota_e", [P, E])
        tok_p = sb("tok_p", [P, 1])
        tok_j = sb("tok_j", [P, B])
        dump = sb("dump", [P, 1])
        one_c = sb("one_c", [P, 1])
        zrow = sb("zrow", [P, H])

        st = sb("st", [P, B, 6])
        mv = sb("mv", [P, B, 2])
        gates = sb("gates", [P, B, 2, NH])
        logf = sb("logf", [P, BH])
        fcum = sb("fcum", [P, BH])
        amat = sb("amat", [P, BH])
        aT = sb("aT", [BH // 2, S])
        mT = [sb(f"mT{i}", [BH // 2, S]) for i in range(2)]
        mlog = sb("mlog", [P, BH])
        floor = sb("floor", [P, BH])
        cvT = sb("cvT", [P, 512])
        hraw = sb("hraw", [P, 2, NH, DH + 1])
        hh = sb("hh", [P, 2, NH, DH])
        hc = sb("hc", [P, 2, NH, DH])
        s16 = sb("s16", [P, 4, 2 * NH])
        rs = sb("rs", [P, 3, 2 * NH + 2])
        xlT = sb("xlT", [P, H])

        lt = sb("lt", [P, B, E])
        ex = sb("ex", [P, B, E])
        ex2 = sb("ex2", [P, B, E])
        key = sb("key", [P, B, E])
        oh = sb("oh", [P, TOPK, B, E])
        r8 = sb("r8", [P, 8, B])
        wsel = sb("wsel", [P, TOPK, B])
        mask = sb("mask", [P, B, E], BF16)
        cnt = sb("cnt", [P, E])
        ctile = sb("ctile", [P, E, E])
        ntile = sb("ntile", [P, E])
        zero8 = sb("zero8", [P, E])
        etile = sb("etile", [P, E])
        base = sb("base", [P, E])
        slotm = sb("slotm", [P, B, E])
        slotf = sb("slotf", [P, TOPK * B])
        sloti = sb("sloti", [P, 3, TOPK * B], I32)
        srf = sb("srf", [P, 2, TOPK * B])
        wpart = sb("wpart", [P, 3, TOPK * B], BF16)
        wres = sb("wres", [P, 2, TOPK * B])
        tokf = sb("tokf", [P, 2, NT])
        gidx = sb("gidx", [P, NT], I32)
        sidx = sb("sidx", [P, NT], I32)
        wslot = sb("wslot", [P, NT + 1])
        etf = sb("etf", [P, NT])
        eti = sb("eti", [P, NT], I32)

        dflat = dec.rearrange("p a h s -> p (a h s)")
        cflat = ctx_sb.rearrange("p b h -> p (b h)")

        qflat = qbd.rearrange("p a c h s -> p (a c h s)")

        def carve(flat, widths):
            at, got = 0, []
            for w in widths:
                got.append(flat[:, at:at + w])
                at += w
            return got

        *tail, = carve(dflat, [I] * 6)
        sg_sb, h_sb, hT_sb = tail[0:2], tail[2:4], tail[4:6]
        tail = carve(qflat[:, 4096 - 5 * H:], [H] * 5)
        xg_sb = tail
        tail = carve(cflat, [H] * 4)
        xT_sb, y_sb = tail[0:2], tail[2:4]

        NS = TOPK * B
        oh_r, sel, oh_t, ecmp, tab, slotk = carve(
            qflat, [NS * P // 2, NS * SEL * NT // 2, NS * NT // 2, NT * E, SEL * NT, NS * E])
        tab = tab.rearrange("p (g t) -> p g t", g=SEL)
        slotk = slotk.rearrange("p (k b e) -> p k b e", k=TOPK, b=B)
        fa, fu, fl = carve(hc.rearrange("p b h d -> p (b h d)"), [BH] * 3)
        oh_r = oh_r.bitcast(BF16).rearrange("p (n r) -> p n r", n=NS)
        sel = sel.bitcast(BF16).rearrange("p (n g t) -> p n g t", n=NS, g=SEL)
        oh_t = oh_t.bitcast(BF16).rearrange("p (n t) -> p n t", n=NS)
        ecmp = ecmp.rearrange("p (t e) -> p t e", t=NT)

        s_x = [sem(f"x_loaded{i}") for i in range(2)]
        s_c = [sem(f"ctx_loaded{i}") for i in range(2)]
        s_par = sem("params_loaded")
        s_w = sem("experts_loaded")
        s_const = sem("constants_made")
        s_const2 = sem("buffers_cleared")
        s_tg = sem("gains_made")
        s_par2 = sem("params_folded")
        s_rstd0 = sem("var_ready")
        s_xn = sem("xn_ready")
        s_qkt = sem("qk_transposed")
        s_qks = sem("qk_stored")
        s_gate = sem("gates_done")
        s_gT = sem("gates_biased")
        s_gt = sem("gates_turned")
        s_gsb = sem("gates_stored")
        s_lf = sem("softplus_done")
        s_logf = sem("logf_done")
        s_fps = sem("cumsum_done")
        s_a = sem("a_done")
        s_aT = sem("a_transposed")
        s_mT = sem("mprime_done")
        s_m2 = sem("mprime_transposed")
        s_ml = sem("maxlog_done")
        s_fl = sem("floor_done")
        s_mst = [sem(f"mprime_stored{i}") for i in range(2)]
        s_bc = [sem(f"mprime_spread{i}") for i in range(3)]
        s_qbd = [sem(f"q_placed{i}") for i in range(2)]
        s_dm = sem("decay_masked")
        s_dec = sem("decay_done")
        s_vp = sem("v_copied")
        s_sc = sem("scores_done")
        s_cm = sem("c_done")
        s_cv = sem("cv_done")
        s_ots = sem("cvT_stored")
        s_ho = sem("cv_transposed")
        s_hst = sem("cv_stored")
        s_hraw = sem("cv_used")
        s_hn = sem("head_normed")
        s_hs = sem("head_scaled")
        s_rs2 = sem("x2_rstd_done")
        s_x2 = sem("x2_done")
        s_xn2 = sem("xn2_done")
        s_rt = sem("xn2_transposed")
        s_rts = sem("xn2T_stored")
        s_lg = sem("logits_done")
        s_exl = sem("router_exp_done")
        s_mask = sem("mask_done")
        s_rank = sem("ranks_done")
        s_sel = sem("selectors_done")
        s_tab = sem("tables_done")
        s_idx = sem("indices_done")
        s_eti = sem("tile_experts_done")
        s_xno = sem("xn2_written")
        s_x2o = sem("x2_written")
        s_dump = sem("spare_rows_cleared")
        s_xg = [sem(f"tokens_gathered{i}") for i in range(5)]
        s_xt = sem("x_tile_transposed")
        s_xts = sem("x_tile_stored")
        s_gu = sem("gate_up_done")
        s_si = sem("silu_done")
        s_hm = sem("hidden_done")
        s_htp = sem("hidden_transposed")
        s_hts = sem("hiddenT_stored")
        s_y = sem("y_done")
        s_ys = sem("y_scaled")
        s_add = sem("y_added")
        s_vch = sem("vector_step")
        s_sch = sem("scalar_step")
        s_pch = sem("pool_step")

        HB = B // 2
        HBH = BH // 2
        NPAR = 8
        LAG = 6
        NG = B // 2
        GATHER = 5
        x_tok = x.rearrange("b s h -> s b h")
        c_tok = ctx_in.rearrange("b s h -> s b h")

        def w_at(name, k, off=0):
            start = {"w1": 0, "w3": KC * I, "w2": 2 * KC * I}[name]
            width = H if name == "w2" else I
            return start + k * width, width

        block = ctx.enter_context(nc.Block())

        @block.sync
        def _(sp):
            for i in range(2):
                sp.dma_start(x_sb[:, i * HB:(i + 1) * HB, :], x_tok[:, i * HB:(i + 1) * HB, :]).then_inc(s_x[i], 16)
                sp.dma_start(ctx_sb[:, i * HB:(i + 1) * HB, :], c_tok[:, i * HB:(i + 1) * HB, :]).then_inc(s_c[i], 16)

            def experts(e):
                for name, w, parts in (("w1", w1, KC), ("w3", w3, KC), ("w2", w2, IC)):
                    at, width = w_at(name, 0)
                    dst = w_sb[:, e * WE + at:e * WE + at + parts * width].rearrange("p (k n) -> p k n", k=parts)
                    sp.dma_start(dst, w[e].rearrange("(k p) n -> p k n", p=P)).then_inc(s_w, 16)

            def place_q(b):
                sp.wait_ge(s_qks, b + 1)
                if b >= 2:
                    sp.wait_ge(s_sc, KC * (b - 1))
                for h in range(HC):
                    rows = slice(h * DH, (h + 1) * DH)
                    sp.dma_start(qbd[rows, b % 2, :, h, :], qkT[rows, b, 0:KC, :]).then_inc(s_qbd[b % 2], 16)

            def spread_m(b):
                if b >= 3:
                    sp.wait_ge(s_cv, KC * (b - 2))
                sp.dma_start(dec[:, b % 3].rearrange("p h s -> p (h s)"),
                             mprime_dram[b:b + 1, :].to_broadcast([P, NH * S])).then_inc(s_bc[b % 3], 16)

            for e in range(4):
                experts(e)
            sp.wait_ge(s_const2, 2)
            place_q(0)
            place_q(1)
            for i in range(2):
                rows = mprime_dram[i * HB:(i + 1) * HB, :].rearrange("b (h s) -> (b h) s", s=S)
                sp.wait_ge(s_mT, i + 1)
                sp.dma_start(rows, mT[i][:, :]).then_inc(s_mst[i], 16)
                if i == 0:
                    sp.wait_ge(s_mst[0], 16)
                    for b in range(3):
                        spread_m(b)
            sp.wait_ge(s_mst[1], 16)
            for b in range(B):
                if b + 2 < B:
                    place_q(b + 2)
                if b + 3 < B:
                    spread_m(b + 3)
                if b < E - 4:
                    experts(b + 4)
            sp.wait_ge(s_xno, 16 * B)
            sp.wait_ge(s_x2o, 16 * B)
            sp.wait_ge(s_add, 16 * NT)

        @block.gpsimd
        def _(pool):
            nc.gpsimd.memset(ident[:], 0.0).then_inc(s_pch, 1)
            nc.gpsimd.memset(tri[:], 1.0).then_inc(s_pch, 1)
            nc.gpsimd.memset(tri_s[:], 1.0).then_inc(s_pch, 1)
            pool.wait_ge(s_pch, 3)
            nc.gpsimd.affine_select(out=ident[:], in_=ident[:], compare_op=ALU.not_equal, fill=1.0, base=0,
                                    pattern=[[-1, P]], channel_multiplier=1).then_inc(s_const, 1)
            nc.gpsimd.affine_select(out=tri[:], in_=tri[:], compare_op=ALU.is_ge, fill=0.0, base=0,
                                    pattern=[[1, P]], channel_multiplier=-1).then_inc(s_const, 1)
            nc.gpsimd.affine_select(out=tri_s[:], in_=tri_s[:], compare_op=ALU.is_gt, fill=0.0, base=0,
                                    pattern=[[1, P]], channel_multiplier=-1).then_inc(s_const, 1)
            nc.gpsimd.memset(vp[:], 0.0).then_inc(s_pch, 1)
            nc.gpsimd.memset(qbd[:], 0.0).then_inc(s_const2, 1)
            nc.gpsimd.memset(ones_b[:], 1.0).then_inc(s_const, 1)
            nc.gpsimd.memset(zrow[:], 0.0).then_inc(s_const, 1)
            nc.gpsimd.memset(zero8[:], 0.0).then_inc(s_const, 1)
            nc.gpsimd.iota(iota_r[:], [[1, P]], base=0, channel_multiplier=0,
                           allow_small_or_imprecise_dtypes=True).then_inc(s_const, 1)
            nc.gpsimd.iota(iota_t[:], [[1, NT]], base=0, channel_multiplier=0,
                           allow_small_or_imprecise_dtypes=True).then_inc(s_const, 1)
            nc.gpsimd.iota(iota_c[:], [[P, E]], base=0, channel_multiplier=0,
                           allow_small_or_imprecise_dtypes=True).then_inc(s_const, 1)
            nc.gpsimd.iota(iota_e[:], [[-1, E]], base=E, channel_multiplier=0,
                           allow_small_or_imprecise_dtypes=True).then_inc(s_const, 1)
            nc.gpsimd.iota(tok_p[:], [[0, 1]], base=0, channel_multiplier=1,
                           allow_small_or_imprecise_dtypes=True).then_inc(s_const, 1)
            nc.gpsimd.iota(tok_j[:], [[S, B]], base=0, channel_multiplier=0,
                           allow_small_or_imprecise_dtypes=True).then_inc(s_const, 1)
            nc.gpsimd.iota(dump[:], [[0, 1]], base=T, channel_multiplier=1,
                           allow_small_or_imprecise_dtypes=True).then_inc(s_const, 1)
            pool.wait_ge(s_pch, 4)
            nc.gpsimd.memset(vp[:, :, :, DH:DH + 1], 1.0).then_inc(s_const2, 1)
            pool.wait_ge(s_const, 13)
            pool.dma_start(out[T:T + P, :], zrow[:, :]).then_inc(s_dump, 16)

            def mask_decay(b):
                pool.wait_ge(s_bc[b % 3], 16 * (b // 3 + 1))
                for c in range(KC):
                    v = dec[:, b % 3, c * HC:(c + 1) * HC, :]
                    nc.gpsimd.affine_select(out=v, in_=v, compare_op=ALU.is_ge, fill=BIG, base=0,
                                            pattern=[[0, HC], [1, S]], channel_multiplier=-1).then_inc(s_dm, 1)

            def norm_x2(g):
                pool.wait_ge(s_rs2, g + 1)
                for b in (2 * g, 2 * g + 1):
                    nc.gpsimd.tensor_scalar(xn_sb[:, b, :], x_sb[:, b, :], mv[:, b, 0:1], rstd2[:, b:b + 1],
                                            ALU.subtract, ALU.mult).then_inc(s_xn2, 1)

            def add_heads(g):
                pool.wait_ge(s_hn, g + 1)
                hv = hh.rearrange("p b h d -> p b (h d)")
                nc.gpsimd.tensor_tensor(hv, hv, lns[:, :].unsqueeze(1).to_broadcast([P, 2, H]),
                                        ALU.mult).then_inc(s_hs, 1)
                pool.wait_ge(s_hs, g + 1)
                xv = x_sb[:, 2 * g:2 * g + 2, :]
                nc.gpsimd.tensor_tensor(xv, xv, hv, ALU.add).then_inc(s_x2, 1)

            mask_decay(0)
            mask_decay(1)
            pool.wait_ge(s_par2, 2)
            for b in range(B + 1):
                if b + 2 < B:
                    mask_decay(b + 2)
                if b >= 3 and b % 2 == 1:
                    g = (b - 3) // 2
                    if g >= 1:
                        norm_x2(g - 1)
                    add_heads(g)
            norm_x2(NG - 2)
            add_heads(NG - 1)
            norm_x2(NG - 1)

            def gather(i):
                if i >= GATHER:
                    pool.wait_ge(s_xt, i - GATHER + 1)
                nc.gpsimd.indirect_dma_start(
                    out=xg_sb[i % GATHER], out_offset=None, in_=xn_dram[:, :],
                    in_offset=bass.IndirectOffsetOnAxis(ap=gidx[:, i:i + 1], axis=0)).then_inc(s_xg[i % GATHER], 16)

            pool.wait_ge(s_idx, 1)
            pool.wait_ge(s_xno, 16 * B)
            for i in range(GATHER - 1):
                gather(i)
            pool.wait_ge(s_x2o, 16 * B)
            pool.wait_ge(s_dump, 16)
            for i in range(NT):
                if i + GATHER - 1 < NT:
                    gather(i + GATHER - 1)
                pool.wait_ge(s_ys, i + 1)
                if i >= 1:
                    pool.wait_ge(s_add, 16 * i)
                nc.gpsimd.indirect_dma_start(
                    out=out[:, :], out_offset=bass.IndirectOffsetOnAxis(ap=sidx[:, i:i + 1], axis=0),
                    in_=y_sb[i % 2], in_offset=None, compute_op=ALU.add).then_inc(s_add, 16)
            pool.wait_ge(s_add, 16 * NT)

        @block.scalar
        def _(act):
            act.dma_start(gx[:, 0:1], g_xattn.rearrange("(a b) -> a b", a=1).to_broadcast([P, 1])).then_inc(s_par, 16)
            act.dma_start(gx[:, 1:2], g_ffn.rearrange("(a b) -> a b", a=1).to_broadcast([P, 1])).then_inc(s_par, 16)
            act.dma_start(wg_sb[:, :, 0:NH], wi.rearrange("(c p) h -> p c h", p=P)).then_inc(s_par, 16)
            act.dma_start(wg_sb[:, :, NH:G2], wf.rearrange("(c p) h -> p c h", p=P)).then_inc(s_par, 16)
            act.dma_start(gb_sb[0:NH, :], bi.rearrange("(h a) -> h a", a=1)).then_inc(s_par, 16)
            act.dma_start(gb_sb[NH:G2, :], bf.rearrange("(h a) -> h a", a=1)).then_inc(s_par, 16)
            act.dma_start(lns[:], ln_scale.rearrange("(a h) -> a h", a=1).to_broadcast([P, H])).then_inc(s_par, 16)
            act.dma_start(wr_sb[:], w_gate.rearrange("(c p) e -> p c e", p=P)).then_inc(s_par, 16)
            act.wait_ge(s_par, 16 * NPAR)
            nc.scalar.activation(tg[:], gx[:], ACT.Tanh).then_inc(s_tg, 1)

            nc.scalar.preload_act_table_set("natural_log_exp_and_others")

            v3 = lambda t: t.rearrange("p (b h) -> p b h", b=HB)
            for i in range(2):
                for b in range(i * HB, (i + 1) * HB):
                    act.wait_ge(s_qkt, b + 1)
                    nc.scalar.activation(qkT[:, b].rearrange("p c s -> p (c s)"), ps_scores[0][:, b % 2, :],
                                         ACT.Copy).then_inc(s_qks, 1)
            for i in range(2):
                hb = slice(i * HBH, (i + 1) * HBH)
                act.wait_ge(s_gsb, i + 1)
                nc.scalar.activation(v3(fa[:, hb]), gates[:, i * HB:(i + 1) * HB, 1, :], ACT.Abs).then_inc(s_sch, 1)
                act.wait_ge(s_sch, 2 * i + 1)
                nc.scalar.activation(fu[:, hb], fa[:, hb], ACT.Exp, scale=-1.0).then_inc(s_sch, 1)
                act.wait_ge(s_sch, 2 * i + 2)
                if i == 0:
                    act.wait_ge(s_const2, 3)
                nc.scalar.activation(fl[:, hb], fu[:, hb], ACT.Ln, bias=one_c[:, 0:1]).then_inc(s_lf, 1)
            for i in range(2):
                hb = slice(i * HBH, (i + 1) * HBH)
                act.wait_ge(s_ml, i + 1)
                nc.scalar.activation(floor[:, hb], mlog[:, hb], ACT.Exp, scale=-1.0).then_inc(s_fl, 1)

            def copy_v(b):
                if b >= 2:
                    act.wait_ge(s_cv, KC * (b - 1))
                nc.scalar.activation(vp[:, b % 2, :, 0:DH], ctx_sb[:, b].rearrange("p (h d) -> p h d", h=NH),
                                     ACT.Copy).then_inc(s_vp, 1)

            def decay(b, c):
                act.wait_ge(s_dm, KC * b + c + 1)
                for h in range(c * HC, (c + 1) * HC):
                    d = dec[:, b % 3, h, :]
                    last = nc.scalar.activation(d, d, ACT.Exp, bias=amat[:, b * NH + h:b * NH + h + 1], scale=-1.0)
                last.then_inc(s_dec, 1)

            def store_cvT(b):
                act.wait_ge(s_cv, KC * (b + 1))
                if b >= 1:
                    act.wait_ge(s_ho, b)
                nc.scalar.activation(cvT[:], ps_ht[:, :], ACT.Copy).then_inc(s_ots, 1)

            def store_cv(b):
                act.wait_ge(s_ho, b + 1)
                if b >= 2:
                    act.wait_ge(s_hraw, b // 2)
                nc.scalar.activation(hraw[:, b % 2], ps_h.rearrange("p (h v) -> p h v", v=VW)[:, :, 0:DH + 1],
                                     ACT.Copy).then_inc(s_hst, 1)

            def store_xnT(b):
                act.wait_ge(s_rt, b + 1)
                act.dma_start(xn_dram[b * S:(b + 1) * S, :], xn_sb[:, b, :]).then_inc(s_xno, 16)
                act.dma_start(out[b * S:(b + 1) * S, :], x_sb[:, b, :]).then_inc(s_x2o, 16)
                if b >= 1:
                    act.wait_ge(s_lg, b)
                nc.scalar.activation(xlT[:], ps_tr[:, 0:H], ACT.Copy).then_inc(s_rts, 1)

            act.wait_ge(s_const2, 2)
            act.wait_ge(s_c[0], 16)
            act.wait_ge(s_c[1], 16)
            copy_v(0)
            decay(0, 0)
            decay(0, 1)
            for b in range(B):
                if b + 1 < B:
                    decay(b + 1, 0)
                if b >= 1:
                    store_cv(b - 1)
                if b + 1 < B:
                    copy_v(b + 1)
                    decay(b + 1, 1)
                if b >= LAG:
                    store_xnT(b - LAG)
                store_cvT(b)
            store_cv(B - 1)
            nc.scalar.preload_act_table_set("exp_and_others")
            for b in range(B - LAG, B):
                store_xnT(b)

            act.wait_ge(s_lg, B)
            nc.scalar.activation(lt.rearrange("p b e -> p (b e)"), ps_small[:, 0:B * E], ACT.Tanh,
                                 scale=1.0 / SOFTCAP).then_inc(s_sch, 1)
            act.wait_ge(s_sch, 5)
            nc.scalar.activation(ex[:], lt[:], ACT.Exp, scale=SOFTCAP).then_inc(s_exl, 1)
            nc.scalar.preload_act_table_set("silu_and_others")

            def silu(i, p):
                act.wait_ge(s_gu, i + 1)
                nc.scalar.activation(sg_sb[p], ps_scores[p][:, 0, :], ACT.Silu).then_inc(s_si, 1)

            def store_hT(i, p):
                act.wait_ge(s_htp, i + 1)
                nc.scalar.activation(hT_sb[p], ps_ht[:, :], ACT.Copy).then_inc(s_hts, 1)

            silu(0, 0)
            with act.Fori(0, NT - 1, 2) as i:
                store_hT(i, 0)
                silu(i + 1, 1)
                store_hT(i + 1, 1)
                silu(i + 2, 0)
            store_hT(NT - 1, 0)

        @block.vector
        def _(dve):
            chain = [0]

            def link(ins):
                chain[0] += 1
                ins.then_inc(s_vch, 1)
                dve.wait_ge(s_vch, chain[0])

            def rsqrt(y, v, t):
                yi, vi = y.bitcast(I32), v.bitcast(I32)
                link(nc.vector.tensor_scalar(yi, vi, 1, None, ALU.logical_shift_right))
                link(nc.vector.tensor_scalar(yi, yi, -1.0, float(RSQRT_MAGIC), ALU.mult, ALU.add))
                for _ in range(3):
                    link(nc.vector.tensor_tensor(t, y, y, ALU.mult))
                    link(nc.vector.scalar_tensor_tensor(out=t, in0=t, scalar=-0.5, in1=v, op0=ALU.mult, op1=ALU.mult))
                    link(nc.vector.scalar_tensor_tensor(out=y, in0=t, scalar=1.5, in1=y, op0=ALU.add, op1=ALU.mult))

            nc.vector.memset(one_c[:], 1.0).then_inc(s_const2, 1)
            for i in range(2):
                dve.wait_ge(s_x[i], 16)
                for b in range(i * HB, (i + 1) * HB):
                    nc.vector.bn_stats(st[:, b, :], x_sb[:, b, :]).then_inc(s_vch, 1)
                    chain[0] += 1
                dve.wait_ge(s_vch, chain[0])
                for b in range(i * HB, (i + 1) * HB):
                    nc.vector.bn_aggr(mv[:, b, :], st[:, b, :]).then_inc(s_vch, 1)
                    chain[0] += 1
                dve.wait_ge(s_vch, chain[0])
                hb = slice(i * HB, (i + 1) * HB)
                link(nc.vector.tensor_scalar(rs[:, 0, 0:HB], mv[:, hb, 1], LN_EPS, None, ALU.add))
                rsqrt(rs[:, 1, 0:HB], rs[:, 0, 0:HB], rs[:, 2, 0:HB])
                for b in range(i * HB, (i + 1) * HB):
                    k = b - i * HB
                    nc.vector.tensor_scalar(xn_sb[:, b, :], x_sb[:, b, :], mv[:, b, 0:1], rs[:, 1, k:k + 1],
                                            ALU.subtract, ALU.mult).then_inc(s_xn, 1)
                if i == 0:
                    dve.wait_ge(s_par, 16 * NPAR)
                    nc.vector.tensor_tensor(wg_sb[:, KC:2 * KC, :], wg_sb[:, KC:2 * KC, :], wg_sb[:, 2 * KC:3 * KC, :],
                                            ALU.add).then_inc(s_par2, 1)
                    dve.wait_ge(s_tg, 1)
                    nc.vector.tensor_scalar(lns[:], lns[:], tg[:, 0:1], None, ALU.mult).then_inc(s_par2, 1)

            v3 = lambda t: t.rearrange("p (b h) -> p b h", b=HB)
            for i in range(2):
                hb = slice(i * HBH, (i + 1) * HBH)
                at = i * 4 * HBH
                dve.wait_ge(s_gate, (i + 1) * HB)
                if i == 1:
                    dve.wait_ge(s_gt, 1)
                nc.vector.tensor_scalar(gT_sb.rearrange("p b s -> p (b s)"), ps_scores[1][0:G2, i, :], gb_sb[:, 0:1],
                                        None, ALU.add).then_inc(s_gT, 1)
                dve.wait_ge(s_gt, i + 1)
                nc.vector.tensor_copy(gates[:, i * HB:(i + 1) * HB].rearrange("p b g h -> p (b g h)"),
                                      ps_small[:, i * 128:(i + 1) * 128]).then_inc(s_gsb, 1)
                dve.wait_ge(s_lf, i + 1)
                nc.vector.scalar_tensor_tensor(out=v3(logf[:, hb]), in0=gates[:, i * HB:(i + 1) * HB, 1, :], scalar=0.0,
                                               in1=v3(fl[:, hb]), op0=ALU.min, op1=ALU.subtract).then_inc(s_logf, 1)
                dve.wait_ge(s_fps, i + 1)
                link(nc.vector.tensor_copy(fcum[:, hb], ps_ht[:, at:at + HBH]))
                nc.vector.tensor_tensor(v3(amat[:, hb]), gates[:, i * HB:(i + 1) * HB, 0, :], v3(fcum[:, hb]),
                                        ALU.subtract).then_inc(s_a, 1)
                dve.wait_ge(s_aT, i + 1)
                link(nc.vector.tensor_copy(aT[:], ps_ht[0:HBH, at + HBH:at + HBH + S]))
                nc.vector.tensor_tensor_scan(mT[i][:], aT[:], aT[:], -3.0e38, ALU.max, ALU.max).then_inc(s_mT, 1)
                dve.wait_ge(s_m2, i + 1)
                nc.vector.tensor_tensor(mlog[:, hb], ps_ht[:, at + 3 * HBH:at + 4 * HBH], fcum[:, hb],
                                        ALU.add).then_inc(s_ml, 1)
            dve.wait_ge(s_fl, 2)
            link(nc.vector.tensor_scalar(floor[:], floor[:], MLSTM_EPS, None, ALU.add))

            def c_mult(b, c):
                dve.wait_ge(s_sc, KC * b + c + 1)
                dve.wait_ge(s_dec, KC * b + c + 1)
                d = dec[:, b % 3, c * HC:(c + 1) * HC, :].rearrange("p h s -> p (h s)")
                nc.vector.scalar_tensor_tensor(out=d, in0=ps_scores[c].rearrange("p a n -> p (a n)"),
                                               scalar=float(DH) ** -0.5, in1=d,
                                               op0=ALU.mult, op1=ALU.mult).then_inc(s_cm, 1)

            NH2 = 2 * NH

            def per_head(t):
                return t.unsqueeze(2).to_broadcast([P, NH2, DH])

            def center_heads(g):
                dve.wait_ge(s_hst, 2 * g + 2)
                raw = hraw.rearrange("p b h v -> p (b h) v")
                n, c, q = raw[:, :, DH], hc.rearrange("p b h d -> p (b h) d"), hh.rearrange("p b h d -> p (b h) d")
                link(nc.vector.scalar_tensor_tensor(out=s16[:, 0, :], in0=n, scalar=-1.0, in1=n,
                                                    op0=ALU.mult, op1=ALU.max))
                link(nc.vector.scalar_tensor_tensor(out=s16[:, 1, :], in0=s16[:, 0, :], scalar=MLSTM_EPS,
                                                    in1=floor[:, g * NH2:(g + 1) * NH2], op0=ALU.add, op1=ALU.max))
                link(nc.vector.reciprocal(s16[:, 2, :], s16[:, 1, :]))
                nc.vector.tensor_tensor(c, raw[:, :, 0:DH], per_head(s16[:, 2, :]), ALU.mult).then_inc(s_hraw, 1)
                dve.wait_ge(s_hraw, g + 1)
                link(nc.vector.tensor_reduce(s16[:, 3, :], c, AX_X, ALU.add))
                link(nc.vector.scalar_tensor_tensor(out=c, in0=per_head(s16[:, 3, :]), scalar=-1.0 / DH, in1=c,
                                                     op0=ALU.mult, op1=ALU.add))
                if g >= 1:
                    dve.wait_ge(s_x2, g)
                link(nc.vector.tensor_tensor(q, c, c, ALU.mult))
                link(nc.vector.tensor_reduce(s16[:, 0, :], q, AX_X, ALU.add))
                link(nc.vector.tensor_scalar(rs[:, 0, 0:NH2], s16[:, 0, :], 1.0 / DH, MLSTM_EPS, ALU.mult, ALU.add))

            def stats_x2(g):
                dve.wait_ge(s_x2, g + 1)
                pair = (2 * g, 2 * g + 1)
                for b in pair:
                    chain[0] += 1
                    nc.vector.bn_stats(st[:, b, :], x_sb[:, b, :]).then_inc(s_vch, 1)
                dve.wait_ge(s_vch, chain[0])
                for b in pair:
                    chain[0] += 1
                    nc.vector.bn_aggr(mv[:, b, :], st[:, b, :]).then_inc(s_vch, 1)
                dve.wait_ge(s_vch, chain[0])
                link(nc.vector.tensor_scalar(rs[:, 0, NH2:], mv[:, 2 * g:2 * g + 2, 1], LN_EPS, None, ALU.add))

            def finish(g, heads, x2):
                cols = slice(0 if heads else NH2, NH2 + 2 if x2 else NH2)
                if x2:
                    stats_x2(g - 1)
                rsqrt(rs[:, 1, cols], rs[:, 0, cols], rs[:, 2, cols])
                if x2:
                    nc.vector.tensor_copy(rstd2[:, 2 * g - 2:2 * g], rs[:, 1, NH2:]).then_inc(s_rs2, 1)
                if heads:
                    nc.vector.tensor_tensor(hh.rearrange("p b h d -> p (b h) d"), hc.rearrange("p b h d -> p (b h) d"),
                                            per_head(rs[:, 1, 0:NH2]), ALU.mult).then_inc(s_hn, 1)

            for b in range(B):
                c_mult(b, 0)
                c_mult(b, 1)
                if b >= 2 and b % 2 == 0:
                    center_heads(b // 2 - 1)
                if b >= 3 and b % 2 == 1:
                    finish((b - 3) // 2, True, b >= 5)
            center_heads(NG - 1)
            finish(NG - 1, True, True)
            finish(NG, False, True)

            be = lambda t: t.unsqueeze(2).to_broadcast([P, B, E])
            rev = iota_e[:, :].unsqueeze(1).to_broadcast([P, B, E])
            dve.wait_ge(s_const, 13)
            dve.wait_ge(s_exl, 1)
            src = ex
            for k in range(TOPK):
                link(nc.vector.tensor_reduce(r8[:, k, :], src[:], AX_X, ALU.max))
                link(nc.vector.tensor_tensor(key[:], src[:], be(r8[:, k, :]), ALU.is_equal))
                link(nc.vector.tensor_tensor(key[:], key[:], rev, ALU.mult))
                link(nc.vector.tensor_reduce(r8[:, 2, :], key[:], AX_X, ALU.max))
                link(nc.vector.tensor_tensor(oh[:, k], key[:], be(r8[:, 2, :]), ALU.is_equal))
                if k == 0:
                    link(nc.vector.scalar_tensor_tensor(out=ex2[:], in0=oh[:, 0], scalar=-BIG, in1=ex[:],
                                                        op0=ALU.mult, op1=ALU.add))
                    src = ex2
            nc.vector.tensor_tensor(mask[:], oh[:, 0], oh[:, 1], ALU.add).then_inc(s_mask, 1)
            link(nc.vector.tensor_reduce(r8[:, 3, :], ex[:], AX_X, ALU.add))
            link(nc.vector.reciprocal(r8[:, 4, :], r8[:, 3, :]))
            link(nc.vector.tensor_scalar(r8[:, 4, :], r8[:, 4, :], tg[:, 1:2], None, ALU.mult))
            link(nc.vector.tensor_tensor(wsel[:], r8[:, 0:TOPK, :],
                                         r8[:, 4, :].unsqueeze(1).to_broadcast([P, TOPK, B]), ALU.mult))
            wf = wsel.rearrange("p k b -> p (k b)")
            link(nc.vector.tensor_copy(wpart[:, 0, :], wf))
            link(nc.vector.tensor_tensor(wres[:, 0, :], wf, wpart[:, 0, :], ALU.subtract))
            link(nc.vector.tensor_copy(wpart[:, 1, :], wres[:, 0, :]))
            link(nc.vector.tensor_tensor(wres[:, 1, :], wres[:, 0, :], wpart[:, 1, :], ALU.subtract))
            link(nc.vector.tensor_copy(wpart[:, 2, :], wres[:, 1, :]))

            dve.wait_ge(s_rank, 1)
            link(nc.vector.tensor_copy(cnt[:], ps_small[:, 192:192 + E]))
            link(nc.vector.tensor_tensor(ctile[:], cnt[:, :].unsqueeze(2).to_broadcast([P, E, E]),
                                         iota_c[:, :].unsqueeze(1).to_broadcast([P, E, E]), ALU.is_gt))
            link(nc.vector.tensor_reduce(ntile[:], ctile[:], AX_X, ALU.add))
            link(nc.vector.tensor_tensor_scan(etile[:], ntile[:], zero8[:], 0.0, ALU.add, ALU.add))
            link(nc.vector.tensor_tensor(base[:], etile[:], ntile[:], ALU.subtract))
            link(nc.vector.tensor_scalar(base[:], base[:], float(P), None, ALU.mult))
            link(nc.vector.tensor_tensor(slotm[:], ps_small[:, 128:128 + B * E].rearrange("p (b e) -> p b e", b=B),
                                         base[:, :].unsqueeze(1).to_broadcast([P, B, E]), ALU.add))
            for k in range(TOPK):
                link(nc.vector.tensor_tensor(slotk[:, k], oh[:, k], slotm[:], ALU.mult))
            link(nc.vector.tensor_reduce(slotf[:], slotk.rearrange("p k b e -> p (k b) e"), AX_X, ALU.add))
            link(nc.vector.tensor_copy(sloti[:, 0, :], slotf[:]))
            link(nc.vector.tensor_scalar(sloti[:, 1, :], sloti[:, 0, :], P - 1, None, ALU.bitwise_and))
            link(nc.vector.tensor_scalar(sloti[:, 2, :], sloti[:, 0, :], 7, None, ALU.logical_shift_right))
            link(nc.vector.tensor_copy(srf[:], sloti[:, 1:3, :]))
            link(nc.vector.tensor_tensor(oh_t[:], iota_t[:, :].unsqueeze(1).to_broadcast([P, NS, NT]),
                                         srf[:, 1, :].unsqueeze(2).to_broadcast([P, NS, NT]), ALU.is_equal))
            tj = tok_j[:, :].unsqueeze(1).to_broadcast([P, TOPK, B])
            link(nc.vector.tensor_copy(wres[:, 0, :].rearrange("p (k b) -> p k b", k=TOPK), tj))
            nt = lambda t: t.unsqueeze(2).to_broadcast([P, NS, NT])
            link(nc.vector.tensor_scalar(sel[:, :, 0, :], oh_t[:], tok_p[:, 0:1], None, ALU.mult))
            link(nc.vector.tensor_tensor(sel[:, :, 1, :], oh_t[:], nt(wres[:, 0, :]), ALU.mult))
            link(nc.vector.tensor_copy(sel[:, :, 2, :], oh_t[:]))
            for j in range(3):
                link(nc.vector.tensor_tensor(sel[:, :, 3 + j, :], oh_t[:], nt(wpart[:, j, :]), ALU.mult))
            nc.vector.tensor_tensor(oh_r[:], iota_r[:, :].unsqueeze(1).to_broadcast([P, NS, P]),
                                    srf[:, 0, :].unsqueeze(2).to_broadcast([P, NS, P]),
                                    ALU.is_equal).then_inc(s_sel, 1)
            link(nc.vector.tensor_tensor(ecmp[:], iota_t[:, :].unsqueeze(2).to_broadcast([P, NT, E]),
                                         etile[:, :].unsqueeze(1).to_broadcast([P, NT, E]), ALU.is_ge))
            link(nc.vector.tensor_reduce(etf[:], ecmp[:], AX_X, ALU.add))
            nc.vector.tensor_scalar(eti[:], etf[:], float(E - 1), None, ALU.min).then_inc(s_eti, 1)

            dve.wait_ge(s_tab, 1)
            link(nc.vector.tensor_copy(tab.rearrange("p g t -> p (g t)"), ps_small[:, 256:256 + SEL * NT]))
            link(nc.vector.tensor_tensor(tokf[:, 0, :], tab[:, 0, :], tab[:, 1, :], ALU.add))
            link(nc.vector.tensor_copy(gidx[:], tokf[:, 0, :]))
            link(nc.vector.tensor_scalar(tokf[:, 1, :], tab[:, 2, :], -1.0, 1.0, ALU.mult, ALU.add))
            link(nc.vector.scalar_tensor_tensor(out=tokf[:, 1, :], in0=tokf[:, 1, :], scalar=dump[:, 0:1],
                                                in1=tokf[:, 0, :], op0=ALU.mult, op1=ALU.add))
            nc.vector.tensor_copy(sidx[:], tokf[:, 1, :]).then_inc(s_idx, 1)
            link(nc.vector.tensor_tensor(wslot[:, 0:NT], tab[:, 3, :], tab[:, 4, :], ALU.add))
            link(nc.vector.tensor_tensor(wslot[:, 0:NT], wslot[:, 0:NT], tab[:, 5, :], ALU.add))

            def store_xT(i, p):
                dve.wait_ge(s_xt, i + 1)
                nc.vector.tensor_copy(xT_sb[p], ps_h[:, 0:H]).then_inc(s_xts, 1)

            def hidden(i, p):
                dve.wait_ge(s_si, i + 1)
                nc.vector.tensor_tensor(h_sb[p], sg_sb[p], ps_scores[p][:, 1, :], ALU.mult).then_inc(s_hm, 1)

            def scale_y(i, p, first=False):
                dve.wait_ge(s_y, i + 1)
                if not first:
                    dve.wait_ge(s_add, 16 * i - 16)
                nc.vector.tensor_scalar(y_sb[p], ps_tr[:, 0:H], wslot[:, bass.ds(i, 1)], None,
                                        ALU.mult).then_inc(s_ys, 1)

            store_xT(0, 0)
            store_xT(1, 1)
            hidden(0, 0)
            store_xT(2, 0)
            hidden(1, 1)
            scale_y(0, 0, True)
            store_xT(3, 1)
            hidden(2, 0)
            scale_y(1, 1, True)
            with dve.Fori(2, NT - 3, 2) as i:
                store_xT(i + 2, 0)
                hidden(i + 1, 1)
                scale_y(i, 0)
                store_xT(i + 3, 1)
                hidden(i + 2, 0)
                scale_y(i + 1, 1)
            store_xT(NT - 1, 0)
            hidden(NT - 2, 1)
            scale_y(NT - 3, 0)
            hidden(NT - 1, 0)
            scale_y(NT - 2, 1)
            scale_y(NT - 1, 0)

        @block.tensor
        def _(pe):
            pe.wait_ge(s_const, 13)
            for b in range(B + 1):
                if b < B:
                    pe.wait_ge(s_xn, b + 1)
                    pe.wait_ge(s_c[b // HB], 16)
                    if b >= 2:
                        pe.wait_ge(s_qks, b - 1)
                    for c in range(KC):
                        nc.tensor.transpose(ps_scores[0][:, b % 2, c * P:(c + 1) * P],
                                            xn_sb[:, b, c * P:(c + 1) * P], ident[:])
                    for c in range(KC):
                        last = nc.tensor.transpose(ps_scores[0][:, b % 2, (KC + c) * P:(KC + c + 1) * P],
                                                   ctx_sb[:, b, c * P:(c + 1) * P], ident[:])
                    last.then_inc(s_qkt, 1)
                if b >= 1:
                    d, i = b - 1, (b - 1) // HB
                    pe.wait_ge(s_qks, b)
                    if b == 1:
                        pe.wait_ge(s_par2, 1)
                    for c in range(2 * KC):
                        last = nc.tensor.matmul(ps_scores[1][0:G2, i, (d % HB) * S:(d % HB + 1) * S], wg_sb[:, c, :],
                                                qkT[:, d, c, :], start=(c == 0), stop=(c == 2 * KC - 1))
                    last.then_inc(s_gate, 1)
            for i in range(2):
                hb = slice(i * HBH, (i + 1) * HBH)
                at = i * 4 * HBH
                pe.wait_ge(s_gT, i + 1)
                if i == 1:
                    pe.wait_ge(s_gsb, 1)
                for b in range(HB):
                    last = nc.tensor.transpose(ps_small[:, i * 128 + b * G2:i * 128 + (b + 1) * G2],
                                               gT_sb[:, b, :], ident[0:G2, 0:G2])
                last.then_inc(s_gt, 1)
                pe.wait_ge(s_logf, i + 1)
                if i == 1:
                    pe.wait_ge(s_ml, 1)
                nc.tensor.matmul(ps_ht[:, at:at + HBH], tri[:], logf[:, hb], start=True, stop=True).then_inc(s_fps, 1)
                pe.wait_ge(s_a, i + 1)
                nc.tensor.transpose(ps_ht[0:HBH, at + HBH:at + HBH + S], amat[:, hb], ident[:]).then_inc(s_aT, 1)
                pe.wait_ge(s_mT, i + 1)
                nc.tensor.transpose(ps_ht[:, at + 3 * HBH:at + 4 * HBH], mT[i][:], ident[0:HBH, 0:HBH]).then_inc(s_m2, 1)

            def scores(b, c):
                if c == 0:
                    pe.wait_ge(s_qbd[b % 2], 16 * HC * (b // 2 + 1))
                if b >= 1:
                    pe.wait_ge(s_cm, KC * (b - 1) + c + 1)
                elif c == 1:
                    pe.wait_ge(s_gT, 2)
                for half in range(2):
                    rhs = qbd[:, b % 2, c, half * 4:(half + 1) * 4, :].rearrange("p h s -> p (h s)")
                    last = nc.tensor.matmul(ps_scores[c][:, half, :], qkT[:, b, KC + c, :], rhs, start=True, stop=True)
                last.then_inc(s_sc, 1)

            def cv(b, c):
                pe.wait_ge(s_cm, KC * b + c + 1)
                if c == 0:
                    pe.wait_ge(s_vp, b + 1)
                    if b >= 1:
                        pe.wait_ge(s_ots, b)
                    else:
                        pe.wait_ge(s_ml, 2)
                for h in range(c * HC, (c + 1) * HC):
                    g, j = h // 4, h % 4
                    last = nc.tensor.matmul(ps_ht[j * VW:(j + 1) * VW, g * P:(g + 1) * P], vp[:, b % 2, h, :],
                                            dec[:, b % 3, h, :], start=True, stop=True, tile_position=(0, j * VW))
                last.then_inc(s_cv, 1)

            def turn_cv(b):
                pe.wait_ge(s_ots, b + 1)
                if b >= 1:
                    pe.wait_ge(s_hst, b)
                for g in range(4):
                    last = nc.tensor.transpose(ps_h[:, g * P:(g + 1) * P], cvT[:, g * P:(g + 1) * P], ident[:])
                last.then_inc(s_ho, 1)

            def turn_x2(b):
                pe.wait_ge(s_xn2, b + 1)
                if b >= 1:
                    pe.wait_ge(s_rts, b)
                for c in range(KC):
                    last = nc.tensor.transpose(ps_tr[:, c * P:(c + 1) * P], xn_sb[:, b, c * P:(c + 1) * P], ident[:])
                last.then_inc(s_rt, 1)

            def logits(b):
                pe.wait_ge(s_rts, b + 1)
                for c in range(KC):
                    last = nc.tensor.matmul(ps_small[:, b * E:(b + 1) * E], xlT[:, c * P:(c + 1) * P], wr_sb[:, c, :],
                                            start=(c == 0), stop=(c == KC - 1))
                last.then_inc(s_lg, 1)

            def route(b):
                turn_x2(b)
                logits(b)

            for b in range(B):
                scores(b, 0)
                if b >= 1:
                    turn_cv(b - 1)
                scores(b, 1)
                cv(b, 0)
                if b >= LAG:
                    turn_x2(b - LAG)
                cv(b, 1)
                if b >= LAG:
                    logits(b - LAG)
            turn_cv(B - 1)
            for b in range(B - LAG, B):
                route(b)

            pe.wait_ge(s_mask, 1)
            NR = B * E
            rank = ps_small[:, 128:128 + NR]
            mk = mask.rearrange("p b e -> p (b e)")
            nc.tensor.matmul(rank, tri_s[:], mk, start=True, stop=True)
            for i in range(B - 1):
                nc.tensor.matmul(rank[:, (i + 1) * E:], ones_b[:],
                                 mask[:, i:i + 1, :].to_broadcast([P, B - 1 - i, E]),
                                 start=False, stop=True, skip_group_check=True)
            for i in range(B):
                last = nc.tensor.matmul(ps_small[:, 192:192 + E], ones_b[:], mk[:, i * E:(i + 1) * E],
                                        start=(i == 0), stop=(i == B - 1), skip_group_check=True)
            last.then_inc(s_rank, 1)
            pe.wait_ge(s_sel, 1)
            for n in range(TOPK * B):
                last = nc.tensor.matmul(ps_small[:, 256:256 + SEL * NT], oh_r[:, n, :],
                                        sel[:, n].rearrange("p g t -> p (g t)"),
                                        start=(n == 0), stop=(n == TOPK * B - 1))
            last.then_inc(s_tab, 1)

            def turn_x(i, slot_sem, n, p3, xts=None):
                pe.wait_ge(slot_sem, n)
                if xts is not None:
                    pe.wait_ge(s_xts, xts)
                for c in range(KC):
                    last = nc.tensor.transpose(ps_h[:, c * P:(c + 1) * P], xg_sb[p3][:, c * P:(c + 1) * P], ident[:])
                last.then_inc(s_xt, 1)

            def expert_of(i):
                return pe.value_load(eti[0:1, bass.ds(i, 1)], min_val=0, max_val=E - 1)

            def gate_up(i, p, e):
                pe.wait_ge(s_xts, i + 1)
                for n, name in enumerate(("w1", "w3")):
                    for k in range(KC):
                        at, width = w_at(name, k)
                        last = nc.tensor.matmul(ps_scores[p][:, n, :], xT_sb[p][:, k * P:(k + 1) * P],
                                                w_sb[:, bass.ds(e * WE + at, width)],
                                                start=(k == 0), stop=(k == KC - 1))
                last.then_inc(s_gu, 1)

            def turn_h(i, p, hts=True):
                pe.wait_ge(s_hm, i + 1)
                if hts:
                    pe.wait_ge(s_hts, i)
                for c in range(IC):
                    last = nc.tensor.transpose(ps_ht[:, c * P:(c + 1) * P], h_sb[p][:, c * P:(c + 1) * P], ident[:])
                last.then_inc(s_htp, 1)

            def down(i, p, e, ys=True):
                pe.wait_ge(s_hts, i + 1)
                if ys:
                    pe.wait_ge(s_ys, i)
                for k in range(IC):
                    at, width = w_at("w2", k)
                    last = nc.tensor.matmul(ps_tr[:, 0:H], hT_sb[p][:, k * P:(k + 1) * P],
                                            w_sb[:, bass.ds(e * WE + at, width)],
                                            start=(k == 0), stop=(k == IC - 1))
                last.then_inc(s_y, 1)

            pe.wait_ge(s_w, 16 * 3 * E)
            pe.wait_ge(s_eti, 1)
            for i in range(NT + 1):
                if i == 0:
                    turn_x(0, s_xg[0], 16, 0)
                if i >= 1:
                    turn_h(i - 1, (i - 1) % 2, i >= 2)
                if i < NT:
                    gate_up(i, i % 2, expert_of(i))
                if i + 1 < NT:
                    turn_x(i + 1, s_xg[(i + 1) % GATHER], 16 * ((i + 1) // GATHER + 1), (i + 1) % GATHER, i + 1)
                if i >= 1:
                    down(i - 1, (i - 1) % 2, expert_of(i - 1), i >= 2)


_INS = ['x', 'ctx_2048', 'g_xattn', 'g_ffn', 'L0_xattn_Wi', 'L0_xattn_bi', 'L0_xattn_Wf', 'L0_xattn_bf',
        'L0_xattn_ln_scale', 'L0_ffn_w_gate', 'L0_ffn_w1', 'L0_ffn_w3', 'L0_ffn_w2']


def kernel(**inputs):
    import numpy as _np
    import concourse.bacc as _bacc
    from concourse import mybir as _mybir
    from concourse.bass_utils import run_bass_kernel_spmd as _run

    nc = _bacc.Bacc("TRN2", target_bir_lowering=False, num_devices=1)
    arrays, args = {}, []
    for name in _INS:
        a = _np.ascontiguousarray(inputs[name])
        arrays[f"in_{name}_dram"] = a
        args.append(nc.dram_tensor(f"in_{name}_dram", a.shape, _mybir.dt.from_np(a.dtype), kind="ExternalInput").ap())
    b, s, h = inputs['x'].shape
    args.append(nc.dram_tensor("out_0_dram", (b * s + 128, h), F32, kind="ExternalOutput").ap())
    bass_gated_mlstm_moe_kernel(nc, *args)
    r = _run(nc, [arrays], core_ids=[0])
    return r.results[0]["out_0_dram"][:b * s].reshape(b, s, h)
```

```python
from contextlib import ExitStack

import concourse.bass as bass
from concourse import mybir

F32 = mybir.dt.float32
BF16 = mybir.dt.bfloat16
F16 = mybir.dt.float16
F32R = mybir.dt.float32r
I32 = mybir.dt.int32
ALU = mybir.AluOpType
ACT = mybir.ActivationFunctionType
AX_X = mybir.AxisListType.X

P = 128
BIG = 1.0e30
LN_EPS = 1e-5
MLSTM_EPS = 1e-6
SOFTCAP = 30.0
RSQRT_MAGIC = 0x5F3759DF


def bass_gated_mlstm_moe_kernel(nc, x, ctx_in, g_xattn, g_ffn, wi, bi, wf, bf, ln_scale, w_gate, w1, w3, w2, out):
    B, S, H = x.shape
    NH = wi.shape[1]
    DH = H // NH
    KC = H // P
    E = w_gate.shape[1]
    I = w1.shape[2]
    IC = I // P
    T = B * S
    TOPK = 2
    HC = NH // KC
    VW = 32
    NT = TOPK * T // P + E - 1
    assert S == P and NT % 2 == 1 and (NT - 1) * P <= TOPK * T + E * (P - 1) < (NT + 1) * P
    G2 = 2 * NH
    BH = B * NH
    GROUPS = ((0, 3), (3, B))
    W13 = 2 * KC * I
    W2 = IC * H
    GATHER = 4
    SPLIT = W13 // I

    mprime_dram = nc.dram_tensor("mprime_scratch", [B, NH * S], F32, kind="Internal").ap()
    xn_dram = nc.dram_tensor("xnorm_scratch", [T, H], F32, kind="Internal").ap()

    with ExitStack() as ctx:
        def sb(name, shape, dt=F32):
            return ctx.enter_context(nc.sbuf_tensor(name, shape, dt))

        def sem(name):
            return ctx.enter_context(nc.semaphore(name))

        bank = [ctx.enter_context(nc.psum_tensor(f"bank{i}", [P, 2, 512] if i < 2 else [P, 512], F32))
                for i in range(6)]
        ps_scores = bank[0:2]
        ps_ht = bank[2]
        ps_h = bank[3]
        ps_tr = bank[4]
        ps_small = bank[5]

        def placed(name, shape):
            at = (nc.sbuf_base + 31) // 32 * 32
            return sb(name, shape), nc.alloc_sbuf_tensor_at(name + "_r", shape, F32R, offset=at)

        w13_sb, w13_r = placed("w13_sb", [P, E * W13])
        w2_sb = sb("w2_sb", [P, E * W2])
        x_sb = sb("x_sb", [P, B, H])
        xn_sb, xn_r = placed("xn_sb", [P, B, H])
        arena, arena_r = placed("arena", [P, E * W13])
        widths = (B * 2 * KC * S, 2 * KC * HC * S, B * H, 3 * NH * S)
        assert sum(widths) == E * W13
        qkT, qbd, ctx_sb, dec = (arena[:, sum(widths[:i]):sum(widths[:i + 1])] for i in range(4))
        qkT = qkT.rearrange("p (b c s) -> p b c s", b=B, s=S)
        qbd = qbd.rearrange("p (a c h s) -> p a c h s", a=2, c=KC, s=S)
        ctx_sb = ctx_sb.rearrange("p (b h) -> p b h", b=B)
        dec = dec.rearrange("p (a h s) -> p a h s", a=3, s=S)
        vp = sb("vp", [P, 2, NH, VW])
        wg_sb = sb("wg_sb", [P, 3 * KC, G2])
        gb_sb = sb("gb_sb", [G2, 1])
        wr_sb = sb("wr_sb", [P, KC, E])
        lns = sb("lns", [P, H])
        gx = sb("gx", [P, 2])
        tg = sb("tg", [P, 2])
        ident = sb("ident", [P, P])
        tri = sb("tri", [P, P])
        rstd2 = sb("rstd2", [P, B])
        tri_s = sb("tri_s", [P, P], BF16)
        ones_b = sb("ones_b", [P, P], BF16)
        iota_r = sb("iota_r", [P, P])
        iota_t = sb("iota_t", [P, NT])
        iota_c = sb("iota_c", [P, E])
        iota_e = sb("iota_e", [P, E])
        tok_id = sb("tok_id", [P, TOPK, B])
        dump = sb("dump", [P, 1])
        one_c = sb("one_c", [P, 1])
        zrow = sb("zrow", [P, H])

        st = sb("st", [P, B, 6])
        mv = sb("mv", [P, B, 2])
        gates = sb("gates", [P, B, 2, NH])
        logf = sb("logf", [P, BH])
        fcum = sb("fcum", [P, BH])
        amat = sb("amat", [P, BH])
        GBH = [(b1 - b0) * NH for b0, b1 in GROUPS]
        aT = sb("aT", [max(GBH), S])
        mT = [sb(f"mT{i}", [GBH[i], S]) for i in range(2)]
        mlog = sb("mlog", [P, BH])
        floor = sb("floor", [P, BH])
        cvT = sb("cvT", [P, 512])
        hraw = sb("hraw", [P, 2, NH, DH + 1])
        hh = sb("hh", [P, 2, NH, DH])
        hc = sb("hc", [P, 2, NH, DH])
        s16 = sb("s16", [P, 4, 2 * NH])
        rs = sb("rs", [P, 3, 2 * NH + 2])
        xlT = sb("xlT", [P, 2 * H])

        lt = sb("lt", [P, B, E])
        ex = sb("ex", [P, B, E])
        ex2 = sb("ex2", [P, B, E])
        key = sb("key", [P, B, E])
        oh = sb("oh", [P, TOPK, B, E])
        r8 = sb("r8", [P, 8, B])
        wsel = sb("wsel", [P, TOPK, B])
        mask = sb("mask", [P, B, E], BF16)
        ctile = sb("ctile", [P, E, E])
        ntile = sb("ntile", [P, 1 + E])
        zeros = sb("zeros", [P, 1 + E])
        starts = sb("starts", [P, 1 + E])
        slotm = sb("slotm", [P, B, E])
        sloti = sb("sloti", [P, 3, TOPK * B], I32)
        wpart = sb("wpart", [P, 3, TOPK * B], BF16)
        wres = sb("wres", [P, 2, TOPK * B])
        tokf = sb("tokf", [P, 2, NT])
        gidx = sb("gidx", [P, NT], I32)
        sidx = sb("sidx", [P, NT], I32)
        wslot = sb("wslot", [P, NT + 1])
        etf = sb("etf", [P, NT])
        tab = sb("tab", [P, 5, NT])
        eti = sb("eti", [P, NT], I32)

        def carve(flat, widths):
            at, got = 0, []
            for w in widths:
                got.append(flat[:, at:at + w])
                at += w
            return got

        NS = TOPK * B
        vflat = vp.rearrange("p b h v -> p (b h v)")
        xflat = x_sb.rearrange("p b h -> p (b h)")
        nflat = xn_sb.rearrange("p b h -> p (b h)")
        hcflat = hc.rearrange("p b h d -> p (b h d)")
        hhflat = hh.rearrange("p b h d -> p (b h d)")
        sel, wsl, ecmp, slotk = carve(xflat, [NS * 2 * NT // 2, NS * 3 * NT // 2, NT * E, NS * E])
        *tail, = carve(xflat, [I] * 4)
        sg_sb, h_sb = tail[0:2], tail[2:4]
        xhT_sb, xlT_sb = ([xn_r[:, 2 * part + p, :] for p in range(2)] for part in range(2))
        hT_sb = carve(nflat[:, 4 * H:], [I] * 2)
        xg_sb = carve(cvT, [H] * 2) + carve(hcflat, [H] * 2) + carve(hhflat, [H] * 2)
        y_sb = carve(hraw.rearrange("p b h v -> p (b h v)"), [H] * 2)
        oh_r = vflat[:, 0:NS * P // 2].bitcast(F16).rearrange("p (n r) -> p n r", n=NS)
        sel = sel.bitcast(F16).rearrange("p (n g t) -> p n g t", n=NS, g=2)
        wsl = wsl.bitcast(BF16).rearrange("p (n g t) -> p n g t", n=NS, g=3)
        ecmp = ecmp.rearrange("p (t e) -> p t e", t=NT)
        slotk = slotk.rearrange("p (k b e) -> p k b e", k=TOPK, b=B)
        fa, fu, fl = carve(hcflat, [BH] * 3)

        gT_parts = ((0, 3, xlT), (3, 7, cvT), (7, 8, hhflat))

        s_x = [sem(f"x_loaded{i}") for i in range(2)]
        s_c = [sem(f"ctx_loaded{i}") for i in range(2)]
        s_g = sem("gains_loaded")
        s_par = sem("params_loaded")
        s_w = [sem("first_experts_loaded"), sem("last_experts_loaded")]
        s_ones = sem("ones_made")
        s_const = sem("constants_made")
        s_const2 = sem("buffers_cleared")
        s_tg = sem("gains_made")
        s_par2 = sem("params_folded")
        s_xn = sem("xn_ready")
        s_qkt = sem("qk_transposed")
        s_qks = sem("qk_stored")
        s_gate = sem("gates_done")
        s_gT = sem("gates_biased")
        s_gt = sem("gates_turned")
        s_gsb = sem("gates_stored")
        s_lf = sem("softplus_done")
        s_logf = sem("logf_done")
        s_fps = sem("cumsum_done")
        s_a = sem("a_done")
        s_aT = sem("a_transposed")
        s_mT = sem("mprime_done")
        s_m2 = sem("mprime_transposed")
        s_ml = sem("maxlog_done")
        s_fl = sem("floor_done")
        s_mst = [sem(f"mprime_stored{i}") for i in range(2)]
        s_bc = [[sem(f"mprime_spread{i}{c}") for c in range(KC)] for i in range(3)]
        s_qbd = [sem(f"q_placed{i}") for i in range(2)]
        s_dm = sem("decay_masked")
        s_dec = sem("decay_done")
        s_vc = sem("v_centered")
        s_vp = sem("v_copied")
        s_sc = sem("scores_done")
        s_cm = sem("c_done")
        s_cv = sem("cv_done")
        s_ots = sem("cvT_stored")
        s_ho = sem("cv_transposed")
        s_hst = sem("cv_stored")
        s_hraw = sem("cv_used")
        s_hn = sem("head_normed")
        s_hs = sem("head_scaled")
        s_var = sem("variance_ready")
        s_ry = sem("rsqrt_guess_ready")
        s_x2 = sem("x2_done")
        s_xn2 = sem("xn2_done")
        s_rt = sem("xn2_transposed")
        s_rts = sem("xn2T_stored")
        s_lg = sem("logits_done")
        s_exl = sem("router_exp_done")
        s_mask = sem("mask_done")
        s_rank = sem("ranks_done")
        s_sel = sem("selectors_done")
        s_tab = sem("tables_done")
        s_wsl = sem("weight_selectors_done")
        s_wtab = sem("weight_table_done")
        s_gidx = sem("gather_indices_done")
        s_idx = sem("indices_done")
        s_eti = sem("tile_experts_done")
        s_xno = sem("xn2_written")
        s_x2o = sem("x2_written")
        s_dump = sem("spare_rows_cleared")
        s_xg = [sem(f"tokens_gathered{i}") for i in range(GATHER)]
        s_xt = sem("x_tile_transposed")
        s_wh = sem("upper_weights_made")
        s_wl = sem("lower_weights_made")
        s_xh = sem("x_tile_upper_made")
        s_xts = sem("x_tile_lower_made")
        s_gu = sem("gate_up_done")
        s_si = sem("silu_done")
        s_hm = sem("hidden_done")
        s_htp = sem("hidden_transposed")
        s_hts = sem("hiddenT_stored")
        s_y = sem("y_done")
        s_ys = sem("y_scaled")
        s_add = sem("y_added")
        s_vch = sem("vector_step")
        s_sch = sem("scalar_step")
        s_pch = sem("pool_step")

        HB = B // 2
        NPAR = 6
        NG = B // 2

        def head_cols(g):
            return slice(0, 2 * NH + 2 if g >= 1 else 2 * NH)

        LATE = 4
        x_tok = x.rearrange("b s h -> s b h")
        c_tok = ctx_in.rearrange("b s h -> s b h")

        ht_at = [0, 2 * GBH[0] + S]

        def gate_cols(b, w):
            half, at = (0, min(b, 3) * S) if b in (0, 1, 2, 7) else (1, (b - 3) * S)
            return ps_scores[1][0:G2, half, at:at + w]

        block = ctx.enter_context(nc.Block())

        @block.sync
        def _(sp):
            for i, (b0, b1) in enumerate(GROUPS):
                sp.dma_start(x_sb[:, b0:b1, :], x_tok[:, b0:b1, :]).then_inc(s_x[i], 16)
                sp.dma_start(ctx_sb[:, b0:b1, :], c_tok[:, b0:b1, :]).then_inc(s_c[i], 16)
                if i == 0:
                    sp.dma_start(gb_sb[0:NH, :], bi.rearrange("(h a) -> h a", a=1)).then_inc(s_par, 16)
                    sp.dma_start(gb_sb[NH:G2, :], bf.rearrange("(h a) -> h a", a=1)).then_inc(s_par, 16)
                    sp.dma_start(lns[:], ln_scale.rearrange("(a h) -> a h", a=1).to_broadcast([P, H])).then_inc(
                        s_par, 16)
                    sp.dma_start(wr_sb[:], w_gate.rearrange("(c p) e -> p c e", p=P)).then_inc(s_par, 16)

            def experts(e):
                for w, dst, at, parts, n in ((w1, w13_sb, e * W13, KC, I), (w3, w13_sb, e * W13 + KC * I, KC, I),
                                             (w2, w2_sb, e * W2, IC, H)):
                    dst = dst[:, at:at + parts * n].rearrange("p (k n) -> p k n", k=parts)
                    sp.dma_start(dst, w[e].rearrange("(k p) n -> p k n", p=P)).then_inc(s_w[e >= E - LATE], 16)

            def place_q(b):
                sp.wait_ge(s_qks, b + 1)
                if b >= 2:
                    sp.wait_ge(s_sc, KC * (b - 1))
                for h in range(HC):
                    rows = slice(h * DH, (h + 1) * DH)
                    sp.dma_start(qbd[rows, b % 2, :, h, :], qkT[rows, b, 0:KC, :]).then_inc(s_qbd[b % 2], 16)

            def spread_m(b):
                for c in range(KC):
                    if b >= 3:
                        sp.wait_ge(s_cv, KC * (b - 3) + c + 1)
                    sp.dma_start(dec[:, b % 3, c * HC:(c + 1) * HC].rearrange("p h s -> p (h s)"),
                                 mprime_dram[b:b + 1, c * HC * S:(c + 1) * HC * S].to_broadcast(
                                     [P, HC * S])).then_inc(s_bc[b % 3][c], 16)

            sp.wait_ge(s_par, 16 * NPAR)
            for e in range(2):
                experts(e)
            sp.wait_ge(s_const2, 2)
            place_q(0)

            def store_m(i):
                b0, b1 = GROUPS[i]
                rows = mprime_dram[b0:b1, :].rearrange("b (h s) -> (b h) s", s=S)
                sp.wait_ge(s_mT, i + 1)
                sp.dma_start(rows, mT[i][:, :]).then_inc(s_mst[i], 16)

            store_m(0)
            sp.wait_ge(s_mst[0], 16)
            spread_m(0)
            place_q(1)
            spread_m(1)
            spread_m(2)
            store_m(1)
            experts(2)
            place_q(2)
            sp.wait_ge(s_mst[1], 16)
            for b in range(B):
                if 1 <= b < B - 2:
                    place_q(b + 2)
                if b + 3 < B:
                    spread_m(b + 3)
                if b < E - LATE - 3:
                    experts(b + 3)
            for e in range(E - LATE, E):
                experts(e)
            for b in range(B):
                sp.wait_ge(s_xn2, b + 1)
                sp.dma_start(xn_dram[b * S:(b + 1) * S, :], xn_sb[:, b, :]).then_inc(s_xno, 16)
                sp.dma_start(out[b * S:(b + 1) * S, :], x_sb[:, b, :]).then_inc(s_x2o, 16)
            sp.wait_ge(s_xno, 16 * B)
            sp.wait_ge(s_x2o, 16 * B)
            sp.wait_ge(s_add, 16 * NT)

        @block.gpsimd
        def _(pool):
            nc.gpsimd.memset(ones_b[:], 1.0).then_inc(s_ones, 1)
            nc.gpsimd.memset(ident[:], 0.0).then_inc(s_pch, 1)
            nc.gpsimd.memset(tri[:], 1.0).then_inc(s_pch, 1)
            nc.gpsimd.memset(tri_s[:], 1.0).then_inc(s_pch, 1)
            pool.wait_ge(s_pch, 3)
            nc.gpsimd.affine_select(out=ident[:], in_=ident[:], compare_op=ALU.not_equal, fill=1.0, base=0,
                                    pattern=[[-1, P]], channel_multiplier=1).then_inc(s_const, 1)
            nc.gpsimd.affine_select(out=tri[:], in_=tri[:], compare_op=ALU.is_ge, fill=0.0, base=0,
                                    pattern=[[1, P]], channel_multiplier=-1).then_inc(s_const, 1)
            nc.gpsimd.affine_select(out=tri_s[:], in_=tri_s[:], compare_op=ALU.is_gt, fill=0.0, base=0,
                                    pattern=[[1, P]], channel_multiplier=-1).then_inc(s_const, 1)
            nc.gpsimd.memset(vp[:], 0.0).then_inc(s_pch, 1)
            nc.gpsimd.memset(qbd[:], 0.0).then_inc(s_const2, 1)
            nc.gpsimd.memset(zrow[:], 0.0).then_inc(s_const, 1)
            nc.gpsimd.memset(zeros[:], 0.0).then_inc(s_const, 1)
            nc.gpsimd.iota(iota_r[:], [[1, P]], base=0, channel_multiplier=0,
                           allow_small_or_imprecise_dtypes=True).then_inc(s_const, 1)
            nc.gpsimd.iota(iota_t[:], [[1, NT]], base=0, channel_multiplier=0,
                           allow_small_or_imprecise_dtypes=True).then_inc(s_const, 1)
            nc.gpsimd.iota(iota_c[:], [[P, E]], base=0, channel_multiplier=0,
                           allow_small_or_imprecise_dtypes=True).then_inc(s_const, 1)
            nc.gpsimd.iota(iota_e[:], [[-1, E]], base=E, channel_multiplier=0,
                           allow_small_or_imprecise_dtypes=True).then_inc(s_const, 1)
            nc.gpsimd.iota(tok_id[:], [[0, TOPK], [S, B]], base=0, channel_multiplier=1,
                           allow_small_or_imprecise_dtypes=True).then_inc(s_const, 1)
            nc.gpsimd.iota(dump[:], [[0, 1]], base=T, channel_multiplier=1,
                           allow_small_or_imprecise_dtypes=True).then_inc(s_const, 1)
            pool.wait_ge(s_pch, 4)
            nc.gpsimd.memset(vp[:, :, :, DH:DH + 1], 1.0).then_inc(s_const2, 1)
            pool.wait_ge(s_const, 11)
            nc.gpsimd.memset(iota_c[:, 0:1], -1.0).then_inc(s_const, 1)
            pool.dma_start(out[T:T + P, :], zrow[:, :]).then_inc(s_dump, 16)

            def mask_decay(b):
                for c in range(KC):
                    pool.wait_ge(s_bc[b % 3][c], 16 * (b // 3 + 1))
                    v = dec[:, b % 3, c * HC:(c + 1) * HC, :]
                    nc.gpsimd.affine_select(out=v, in_=v, compare_op=ALU.is_ge, fill=BIG, base=0,
                                            pattern=[[0, HC], [1, S]], channel_multiplier=-1).then_inc(s_dm, 1)

            def add_heads(g):
                pool.wait_ge(s_hn, g + 1)
                if g == 0:
                    pool.wait_ge(s_par2, 2)
                hv = hh.rearrange("p b h d -> p b (h d)")
                nc.gpsimd.tensor_tensor(hv, hv, lns[:, :].unsqueeze(1).to_broadcast([P, 2, H]),
                                        ALU.mult).then_inc(s_hs, 1)
                pool.wait_ge(s_hs, g + 1)
                xv = x_sb[:, 2 * g:2 * g + 2, :]
                nc.gpsimd.tensor_tensor(xv, xv, hv, ALU.add).then_inc(s_x2, 1)

            def copy_v(b):
                if b == 0 or b == HB:
                    pool.wait_ge(s_vc, b // HB + 1)
                if b >= 2:
                    pool.wait_ge(s_cv, KC * (b - 1))
                nc.gpsimd.tensor_copy(vp[:, b % 2, :, 0:DH],
                                      ctx_sb[:, b].rearrange("p (h d) -> p h d", h=NH)).then_inc(s_vp, 1)

            mask_decay(0)
            mask_decay(1)
            copy_v(0)
            for b in range(B + 1):
                if b + 1 < B:
                    copy_v(b + 1)
                if b + 2 < B:
                    mask_decay(b + 2)
                if b >= 3 and b % 2 == 1:
                    add_heads((b - 3) // 2)

            def gather(i):
                if i >= GATHER:
                    pool.wait_ge(s_xt, i - GATHER + 1)
                nc.gpsimd.indirect_dma_start(
                    out=xg_sb[i % GATHER], out_offset=None, in_=xn_dram[:, :],
                    in_offset=bass.IndirectOffsetOnAxis(ap=gidx[:, i:i + 1], axis=0)).then_inc(s_xg[i % GATHER], 16)

            pool.wait_ge(s_gidx, 1)
            pool.wait_ge(s_xno, 16 * B)
            for i in range(GATHER - 1):
                gather(i)
            pool.wait_ge(s_idx, 1)
            pool.wait_ge(s_x2o, 16 * B)
            pool.wait_ge(s_dump, 16)
            for i in range(NT):
                if i + GATHER - 1 < NT:
                    gather(i + GATHER - 1)
                pool.wait_ge(s_ys, i + 1)
                if i >= 1:
                    pool.wait_ge(s_add, 16 * i)
                nc.gpsimd.indirect_dma_start(
                    out=out[:, :], out_offset=bass.IndirectOffsetOnAxis(ap=sidx[:, i:i + 1], axis=0),
                    in_=y_sb[i % 2], in_offset=None, compute_op=ALU.add).then_inc(s_add, 16)
            pool.wait_ge(s_add, 16 * NT)

        @block.scalar
        def _(act):
            act.dma_start(gx[:, 0:1], g_xattn.rearrange("(a b) -> a b", a=1).to_broadcast([P, 1])).then_inc(s_g, 16)
            act.dma_start(gx[:, 1:2], g_ffn.rearrange("(a b) -> a b", a=1).to_broadcast([P, 1])).then_inc(s_g, 16)
            act.dma_start(wg_sb[:, :, 0:NH], wi.rearrange("(c p) h -> p c h", p=P)).then_inc(s_par, 16)
            act.dma_start(wg_sb[:, :, NH:G2], wf.rearrange("(c p) h -> p c h", p=P)).then_inc(s_par, 16)
            act.wait_ge(s_g, 32)
            nc.scalar.activation(tg[:], gx[:], ACT.Tanh).then_inc(s_tg, 1)
            nc.scalar.preload_act_table_set("natural_log_exp_and_others")

            def store_qk(b):
                act.wait_ge(s_qkt, b + 1)
                nc.scalar.activation(qkT[:, b].rearrange("p c s -> p (c s)"), ps_scores[0][:, b % 2, :],
                                     ACT.Copy).then_inc(s_qks, 1)

            def softplus(i):
                b0, b1 = GROUPS[i]
                hb = slice(b0 * NH, b1 * NH)
                v3 = lambda t: t.rearrange("p (b h) -> p b h", h=NH)
                act.wait_ge(s_gsb, i + 1)
                nc.scalar.activation(v3(fa[:, hb]), gates[:, b0:b1, 1, :], ACT.Abs).then_inc(s_sch, 1)
                act.wait_ge(s_sch, 2 * i + 1)
                nc.scalar.activation(fu[:, hb], fa[:, hb], ACT.Exp, scale=-1.0).then_inc(s_sch, 1)
                act.wait_ge(s_sch, 2 * i + 2)
                if i == 0:
                    act.wait_ge(s_const2, 3)
                nc.scalar.activation(fl[:, hb], fu[:, hb], ACT.Ln, bias=one_c[:, 0:1]).then_inc(s_lf, 1)

            def decay(b, c):
                act.wait_ge(s_dm, KC * b + c + 1)
                for h in range(c * HC, (c + 1) * HC):
                    d = dec[:, b % 3, h, :]
                    last = nc.scalar.activation(d, d, ACT.Exp, bias=amat[:, b * NH + h:b * NH + h + 1], scale=-1.0)
                last.then_inc(s_dec, 1)

            def store_cvT(b):
                act.wait_ge(s_cv, KC * (b + 1))
                if b >= 1:
                    act.wait_ge(s_ho, b)
                nc.scalar.activation(cvT[:], ps_ht[:, :], ACT.Copy).then_inc(s_ots, 1)

            def store_cv(b):
                act.wait_ge(s_ho, b + 1)
                if b >= 2:
                    act.wait_ge(s_hraw, b // 2)
                nc.scalar.activation(hraw[:, b % 2], ps_h.rearrange("p (h v) -> p h v", v=VW)[:, :, 0:DH + 1],
                                     ACT.Copy).then_inc(s_hst, 1)

            def store_xnT(g):
                act.wait_ge(s_rt, g + 1)
                if g >= 1:
                    act.wait_ge(s_lg, g)
                nc.scalar.activation(xlT[:], ps_tr[:, :], ACT.Copy).then_inc(s_rts, 1)

            def guess_rsqrt(n, cols):
                act.wait_ge(s_var, n + 1)
                nc.scalar.activation(rs[:, 2, cols], rs[:, 0, cols], ACT.Ln).then_inc(s_sch, 1)
                act.wait_ge(s_sch, 5 + n)
                nc.scalar.activation(rs[:, 1, cols], rs[:, 2, cols], ACT.Exp, scale=-0.5).then_inc(s_ry, 1)

            for b in range(5):
                store_qk(b)
            softplus(0)
            for b in range(5, B):
                store_qk(b)
            decay(0, 0)
            softplus(1)
            decay(0, 1)
            for i, (b0, b1) in enumerate(GROUPS):
                act.wait_ge(s_ml, i + 1)
                nc.scalar.activation(floor[:, b0 * NH:b1 * NH], mlog[:, b0 * NH:b1 * NH], ACT.Exp,
                                     scale=-1.0).then_inc(s_fl, 1)
            for b in range(B):
                if b + 1 < B:
                    decay(b + 1, 0)
                if b >= 1:
                    store_cv(b - 1)
                if b >= 3 and b % 2 == 1:
                    guess_rsqrt((b - 3) // 2, head_cols((b - 3) // 2))
                if b + 1 < B:
                    decay(b + 1, 1)
                if b == B - 1:
                    store_xnT(0)
                store_cvT(b)
            store_cv(B - 1)

            def upper_weights(e, k):
                nc.scalar.activation(arena_r[:, bass.ds(e * W13 + k * I, I)],
                                     w13_sb[:, bass.ds(e * W13 + k * I, I)], ACT.Copy).then_inc(s_wh, 1)

            store_xnT(1)
            act.wait_ge(s_w[0], 16 * 3 * (E - LATE))
            act.wait_ge(s_sc, KC * B)
            for e in range(2):
                for k in range(SPLIT):
                    upper_weights(e, k)
            guess_rsqrt(NG - 1, head_cols(NG - 1))
            guess_rsqrt(NG, slice(2 * NH, 2 * NH + 2))
            store_xnT(2)
            nc.scalar.preload_act_table_set("exp_and_others")
            store_xnT(3)

            act.wait_ge(s_lg, NG)
            nc.scalar.activation(lt.rearrange("p b e -> p (b e)"), ps_small[:, 0:B * E], ACT.Tanh,
                                 scale=1.0 / SOFTCAP).then_inc(s_sch, 1)
            act.wait_ge(s_sch, 6 + NG)
            nc.scalar.activation(ex[:], lt[:], ACT.Exp, scale=SOFTCAP).then_inc(s_exl, 1)
            nc.scalar.preload_act_table_set("silu_and_others")

            def silu(i, p):
                act.wait_ge(s_gu, i + 1)
                nc.scalar.activation(sg_sb[p], ps_scores[p][:, 0, :], ACT.Silu).then_inc(s_si, 1)

            def store_hT(i, p):
                act.wait_ge(s_htp, i + 1)
                nc.scalar.activation(hT_sb[p], ps_ht[:, :], ACT.Copy).then_inc(s_hts, 1)

            def upper_x(i, p):
                act.wait_ge(s_xt, i + 1)
                nc.scalar.activation(xhT_sb[p], ps_h[:, 0:H], ACT.Copy).then_inc(s_xh, 1)

            act.wait_ge(s_cv, KC * B)
            upper_x(0, 0)
            silu(0, 0)
            upper_x(1, 1)
            act.wait_ge(s_w[1], 16 * 3 * LATE)
            with act.Fori(1, E // 2) as pair:
                for p in range(2):
                    e = 2 * pair + p
                    for k in range(SPLIT):
                        upper_weights(e, k)
                    store_hT(e - 2, p)
                    silu(e - 1, 1 - p)
                    upper_x(e, p)
            with act.Fori(E - 2, NT - 3, 2) as i:
                for p in range(2):
                    store_hT(i + p, p)
                    silu(i + p + 1, 1 - p)
                    upper_x(i + p + 2, p)
            store_hT(NT - 3, 0)
            silu(NT - 2, 1)
            upper_x(NT - 1, 0)
            store_hT(NT - 2, 1)
            silu(NT - 1, 0)
            store_hT(NT - 1, 0)

        @block.vector
        def _(dve):
            chain = [0]

            def link(ins):
                chain[0] += 1
                ins.then_inc(s_vch, 1)
                dve.wait_ge(s_vch, chain[0])

            def rsqrt(y, v, t):
                yi, vi = y.bitcast(I32), v.bitcast(I32)
                link(nc.vector.tensor_scalar(yi, vi, 1, None, ALU.logical_shift_right))
                link(nc.vector.tensor_scalar(yi, yi, -1.0, float(RSQRT_MAGIC), ALU.mult, ALU.add))
                for _ in range(3):
                    link(nc.vector.tensor_tensor(t, y, y, ALU.mult))
                    link(nc.vector.scalar_tensor_tensor(out=t, in0=t, scalar=-0.5, in1=v, op0=ALU.mult, op1=ALU.mult))
                    link(nc.vector.scalar_tensor_tensor(out=y, in0=t, scalar=1.5, in1=y, op0=ALU.add, op1=ALU.mult))

            nc.vector.memset(one_c[:], 1.0).then_inc(s_const2, 1)
            link(nc.vector.memset(ntile[:, 0:1], 0.0))
            for i, (b0, b1) in enumerate(GROUPS):
                n = b1 - b0
                dve.wait_ge(s_x[i], 16)
                for b in range(b0, b1):
                    chain[0] += 1
                    nc.vector.bn_stats(st[:, b, :], x_sb[:, b, :]).then_inc(s_vch, 1)
                dve.wait_ge(s_vch, chain[0])
                for b in range(b0, b1):
                    chain[0] += 1
                    nc.vector.bn_aggr(mv[:, b, :], st[:, b, :]).then_inc(s_vch, 1)
                dve.wait_ge(s_vch, chain[0])
                link(nc.vector.tensor_scalar(rs[:, 0, 0:n], mv[:, b0:b1, 1], LN_EPS, None, ALU.add))
                rsqrt(rs[:, 1, 0:n], rs[:, 0, 0:n], rs[:, 2, 0:n])
                for b in range(b0, b1):
                    k = b - b0
                    nc.vector.tensor_scalar(xn_sb[:, b, :], x_sb[:, b, :], mv[:, b, 0:1], rs[:, 1, k:k + 1],
                                            ALU.subtract, ALU.mult).then_inc(s_xn, 1)
                if i == 0:
                    dve.wait_ge(s_par, 16 * NPAR)
                    nc.vector.tensor_tensor(wg_sb[:, KC:2 * KC, :], wg_sb[:, KC:2 * KC, :], wg_sb[:, 2 * KC:3 * KC, :],
                                            ALU.add).then_inc(s_par2, 1)

            def center_v(half):
                seqs = slice(half * HB, (half + 1) * HB)
                dve.wait_ge(s_qkt, (half + 1) * HB)
                v = ctx_sb[:, seqs].rearrange("p b (h d) -> p (b h) d", h=NH)
                mean = s16.rearrange("p a n -> p (a n)")[:, 0:HB * NH]
                link(nc.vector.tensor_reduce(mean, v, AX_X, ALU.add))
                nc.vector.scalar_tensor_tensor(out=v, in0=mean.unsqueeze(2).to_broadcast([P, HB * NH, DH]),
                                               scalar=-1.0 / DH, in1=v, op0=ALU.mult,
                                               op1=ALU.add).then_inc(s_vc, 1)

            def c_mult(b, c):
                dve.wait_ge(s_sc, KC * b + c + 1)
                dve.wait_ge(s_dec, KC * b + c + 1)
                d = dec[:, b % 3, c * HC:(c + 1) * HC, :].rearrange("p h s -> p (h s)")
                nc.vector.scalar_tensor_tensor(out=d, in0=ps_scores[c].rearrange("p a n -> p (a n)"),
                                               scalar=float(DH) ** -0.5, in1=d,
                                               op0=ALU.mult, op1=ALU.mult).then_inc(s_cm, 1)

            v3 = lambda t: t.rearrange("p (b h) -> p b h", h=NH)
            for i, (b0, b1) in enumerate(GROUPS):
                hb, n = slice(b0 * NH, b1 * NH), GBH[i]
                at = ht_at[i]
                if i == 1:
                    center_v(0)
                dve.wait_ge(s_gate, b1)
                for c0, c1, part in gT_parts[i:2 * i + 1]:
                    w = (c1 - c0) * S
                    nc.vector.tensor_scalar(part[0:G2, 0:w], gate_cols(c0, w), gb_sb[:, 0:1],
                                            None, ALU.add).then_inc(s_gT, 1)
                dve.wait_ge(s_gt, i + 1)
                nc.vector.tensor_copy(gates[:, b0:b1].rearrange("p b g h -> p (b g h)"),
                                      ps_small[:, b0 * G2:b1 * G2]).then_inc(s_gsb, 1)
                dve.wait_ge(s_lf, i + 1)
                nc.vector.scalar_tensor_tensor(out=v3(logf[:, hb]), in0=gates[:, b0:b1, 1, :], scalar=0.0,
                                               in1=v3(fl[:, hb]), op0=ALU.min, op1=ALU.subtract).then_inc(s_logf, 1)
                if i == 1:
                    c_mult(0, 0)
                dve.wait_ge(s_fps, i + 1)
                link(nc.vector.tensor_copy(fcum[:, hb], ps_ht[:, at:at + n]))
                nc.vector.tensor_tensor(v3(amat[:, hb]), gates[:, b0:b1, 0, :], v3(fcum[:, hb]),
                                        ALU.subtract).then_inc(s_a, 1)
                dve.wait_ge(s_aT, i + 1)
                link(nc.vector.tensor_copy(aT[0:n, :], ps_ht[0:n, at + n:at + n + S]))
                nc.vector.tensor_tensor_scan(mT[i][:], aT[0:n, :], aT[0:n, :], -3.0e38,
                                             ALU.max, ALU.max).then_inc(s_mT, 1)
                dve.wait_ge(s_m2, i + 1)
                nc.vector.tensor_tensor(mlog[:, hb], ps_ht[:, at + n + S:at + 2 * n + S], fcum[:, hb],
                                        ALU.add).then_inc(s_ml, 1)
            NH2 = 2 * NH

            def per_head(t):
                return t.unsqueeze(2).to_broadcast([P, NH2, DH])

            def center_heads(g):
                dve.wait_ge(s_hst, 2 * g + 2)
                if g == 0:
                    dve.wait_ge(s_vc, 2)
                raw = hraw.rearrange("p b h v -> p (b h) v")
                n, c, q = raw[:, :, DH], hc.rearrange("p b h d -> p (b h) d"), hh.rearrange("p b h d -> p (b h) d")
                link(nc.vector.scalar_tensor_tensor(out=s16[:, 0, :], in0=n, scalar=-1.0, in1=n,
                                                    op0=ALU.mult, op1=ALU.max))
                link(nc.vector.scalar_tensor_tensor(out=s16[:, 1, :], in0=s16[:, 0, :], scalar=MLSTM_EPS,
                                                    in1=floor[:, g * NH2:(g + 1) * NH2], op0=ALU.add, op1=ALU.max))
                link(nc.vector.reciprocal(s16[:, 2, :], s16[:, 1, :]))
                nc.vector.tensor_tensor(c, raw[:, :, 0:DH], per_head(s16[:, 2, :]), ALU.mult).then_inc(s_hraw, 1)
                dve.wait_ge(s_hraw, g + 1)
                if g >= 1:
                    dve.wait_ge(s_x2, g)
                link(nc.vector.tensor_tensor(q, c, c, ALU.mult))
                link(nc.vector.tensor_reduce(s16[:, 0, :], q, AX_X, ALU.add))
                last = nc.vector.tensor_scalar(rs[:, 0, 0:NH2], s16[:, 0, :], 1.0 / DH, MLSTM_EPS, ALU.mult, ALU.add)
                if g == 0:
                    last.then_inc(s_var, 1)
                else:
                    link(last)
                    stats_x2(g - 1)

            def stats_x2(g):
                dve.wait_ge(s_x2, g + 1)
                pair = (2 * g, 2 * g + 1)
                for b in pair:
                    chain[0] += 1
                    nc.vector.bn_stats(st[:, b, :], x_sb[:, b, :]).then_inc(s_vch, 1)
                dve.wait_ge(s_vch, chain[0])
                for b in pair:
                    chain[0] += 1
                    nc.vector.bn_aggr(mv[:, b, :], st[:, b, :]).then_inc(s_vch, 1)
                dve.wait_ge(s_vch, chain[0])
                nc.vector.tensor_scalar(rs[:, 0, NH2:], mv[:, 2 * g:2 * g + 2, 1], LN_EPS, None,
                                        ALU.add).then_inc(s_var, 1)

            def refine(y, v, t):
                link(nc.vector.tensor_tensor(t, y, y, ALU.mult))
                link(nc.vector.scalar_tensor_tensor(out=t, in0=t, scalar=-0.5, in1=v, op0=ALU.mult, op1=ALU.mult))
                link(nc.vector.scalar_tensor_tensor(out=y, in0=t, scalar=1.5, in1=y, op0=ALU.add, op1=ALU.mult))

            def norm_x2(g):
                for b in (2 * g, 2 * g + 1):
                    k = NH2 + b % 2
                    nc.vector.tensor_scalar(xn_sb[:, b, :], x_sb[:, b, :], mv[:, b, 0:1], rs[:, 1, k:k + 1],
                                            ALU.subtract, ALU.mult).then_inc(s_xn2, 1)

            hflat = hh.rearrange("p b h d -> p (b h) d")
            cflat3 = hc.rearrange("p b h d -> p (b h) d")

            def finish(g):
                cols = head_cols(g)
                dve.wait_ge(s_ry, g + 1)
                refine(rs[:, 1, cols], rs[:, 0, cols], rs[:, 2, cols])
                nc.vector.tensor_tensor(hflat, cflat3, per_head(rs[:, 1, 0:NH2]), ALU.mult).then_inc(s_hn, 1)
                if g >= 1:
                    norm_x2(g - 1)

            for b in range(B):
                if b >= 1:
                    c_mult(b, 0)
                c_mult(b, 1)
                if b == 0:
                    dve.wait_ge(s_tg, 1)
                    nc.vector.tensor_scalar(lns[:], lns[:], tg[:, 0:1], None, ALU.mult).then_inc(s_par2, 1)
                    dve.wait_ge(s_fl, 2)
                    link(nc.vector.tensor_scalar(floor[:], floor[:], MLSTM_EPS, None, ALU.add))
                if b == 1:
                    dve.wait_ge(s_vc, 1)
                    center_v(1)
                if b >= 2 and b % 2 == 0:
                    center_heads(b // 2 - 1)
                if b >= 3 and b % 2 == 1:
                    finish((b - 3) // 2)
            g = NG - 1
            center_heads(g)
            hl = hh.rearrange("p b h d -> p b (h d)")
            link(nc.vector.tensor_tensor(hl, hc.rearrange("p b h d -> p b (h d)"),
                                         lns[:, :].unsqueeze(1).to_broadcast([P, 2, H]), ALU.mult))
            dve.wait_ge(s_ry, g + 1)
            refine(rs[:, 1, :], rs[:, 0, :], rs[:, 2, :])
            link(nc.vector.tensor_tensor(hflat, hflat, per_head(rs[:, 1, 0:NH2]), ALU.mult))
            xv = x_sb[:, 2 * g:2 * g + 2, :]
            nc.vector.tensor_tensor(xv, xv, hl, ALU.add).then_inc(s_x2, 1)
            norm_x2(g - 1)
            stats_x2(g)
            dve.wait_ge(s_ry, g + 2)
            refine(rs[:, 1, NH2:], rs[:, 0, NH2:], rs[:, 2, NH2:])
            norm_x2(g)

            def lower_weights(e, k):
                w = w13_sb[:, bass.ds(e * W13 + k * I, I)]
                dve.wait_ge(s_wh, SPLIT * e + k + 1)
                nc.vector.tensor_tensor(w13_r[:, bass.ds(e * W13 + k * I, I)], w,
                                        arena_r[:, bass.ds(e * W13 + k * I, I)].bitcast(F32),
                                        ALU.subtract).then_inc(s_wl, 1)

            def split(e):
                for k in range(SPLIT):
                    lower_weights(e, k)

            split(0)

            be = lambda t: t.unsqueeze(2).to_broadcast([P, B, E])
            rev = iota_e[:, :].unsqueeze(1).to_broadcast([P, B, E])
            dve.wait_ge(s_const, 12)
            dve.wait_ge(s_exl, 1)
            src = ex
            dve.wait_ge(s_x2o, 16 * B)
            dve.wait_ge(s_xno, 16 * B)
            for k in range(TOPK):
                link(nc.vector.tensor_reduce(r8[:, k, :], src[:], AX_X, ALU.max))
                link(nc.vector.tensor_tensor(key[:], src[:], be(r8[:, k, :]), ALU.is_equal))
                link(nc.vector.tensor_tensor(key[:], key[:], rev, ALU.mult))
                link(nc.vector.tensor_reduce(r8[:, 2, :], key[:], AX_X, ALU.max))
                link(nc.vector.tensor_tensor(oh[:, k], key[:], be(r8[:, 2, :]), ALU.is_equal))
                if k == 0:
                    link(nc.vector.scalar_tensor_tensor(out=ex2[:], in0=oh[:, 0], scalar=-BIG, in1=ex[:],
                                                        op0=ALU.mult, op1=ALU.add))
                    src = ex2
            nc.vector.tensor_tensor(mask[:], oh[:, 0], oh[:, 1], ALU.add).then_inc(s_mask, 1)
            dve.wait_ge(s_rank, 1)
            link(nc.vector.tensor_tensor(ctile[:], ps_small[:, 192:192 + E].unsqueeze(2).to_broadcast([P, E, E]),
                                         iota_c[:, :].unsqueeze(1).to_broadcast([P, E, E]), ALU.is_gt))
            link(nc.vector.tensor_reduce(ntile[:, 1:], ctile[:], AX_X, ALU.add))
            link(nc.vector.tensor_tensor_scan(starts[:], ntile[:], zeros[:], 0.0, ALU.add, ALU.add))
            base, etile = starts[:, 0:E], starts[:, 1:]
            link(nc.vector.scalar_tensor_tensor(out=slotm[:], in0=base.unsqueeze(1).to_broadcast([P, B, E]),
                                                scalar=float(P),
                                                in1=ps_small[:, 128:128 + B * E].rearrange("p (b e) -> p b e", b=B),
                                                op0=ALU.mult, op1=ALU.add))
            link(nc.vector.tensor_tensor(slotk.rearrange("p k b e -> p k (b e)"), oh.rearrange("p k b e -> p k (b e)"),
                                         slotm.rearrange("p b e -> p (b e)").unsqueeze(1).to_broadcast(
                                             [P, TOPK, B * E]), ALU.mult))
            with nc.allow_low_precision(reason="the sum of one whole number and zeros"):
                link(nc.vector.tensor_reduce(sloti[:, 0, :], slotk.rearrange("p k b e -> p (k b) e"), AX_X, ALU.add))
            nc.vector.tensor_scalar(sloti[:, 1, :], sloti[:, 0, :], P - 1, None, ALU.bitwise_and).then_inc(s_vch, 1)
            chain[0] += 1
            link(nc.vector.tensor_scalar(sloti[:, 2, :], sloti[:, 0, :], 7, None, ALU.logical_shift_right))
            nt = lambda t: t.unsqueeze(2).to_broadcast([P, NS, NT])
            link(nc.vector.tensor_tensor(sel[:, :, 1, :], iota_t[:, :].unsqueeze(1).to_broadcast([P, NS, NT]),
                                         nt(sloti[:, 2, :]), ALU.is_equal))
            nc.vector.tensor_tensor(sel[:, :, 0, :], sel[:, :, 1, :], nt(tok_id.rearrange("p k b -> p (k b)")),
                                    ALU.mult).then_inc(s_sel, 1)
            for q in range(4):
                n4 = slice(q * NS // 4, (q + 1) * NS // 4)
                nc.vector.tensor_tensor(oh_r[:, n4], iota_r[:, :].unsqueeze(1).to_broadcast([P, NS // 4, P]),
                                        sloti[:, 1, n4].unsqueeze(2).to_broadcast([P, NS // 4, P]),
                                        ALU.is_equal).then_inc(s_sel, 1)
            dve.wait_ge(s_tab, 1)
            nc.vector.tensor_copy(gidx[:], ps_small[:, 256:256 + NT]).then_inc(s_gidx, 1)
            link(nc.vector.tensor_tensor(ecmp[:], iota_t[:, :].unsqueeze(2).to_broadcast([P, NT, E]),
                                         etile.unsqueeze(1).to_broadcast([P, NT, E]), ALU.is_ge))
            link(nc.vector.tensor_reduce(etf[:], ecmp[:], AX_X, ALU.add))
            nc.vector.tensor_scalar(eti[:], etf[:], float(E - 1), None, ALU.min).then_inc(s_eti, 1)
            link(nc.vector.tensor_reduce(r8[:, 3, :], ex[:], AX_X, ALU.add))
            link(nc.vector.reciprocal(r8[:, 4, :], r8[:, 3, :]))
            link(nc.vector.tensor_scalar(r8[:, 4, :], r8[:, 4, :], tg[:, 1:2], None, ALU.mult))
            link(nc.vector.tensor_tensor(wsel[:], r8[:, 0:TOPK, :],
                                         r8[:, 4, :].unsqueeze(1).to_broadcast([P, TOPK, B]), ALU.mult))
            wf = wsel.rearrange("p k b -> p (k b)")
            link(nc.vector.tensor_copy(wpart[:, 0, :], wf))
            link(nc.vector.tensor_tensor(wres[:, 0, :], wf, wpart[:, 0, :], ALU.subtract))
            link(nc.vector.tensor_copy(wpart[:, 1, :], wres[:, 0, :]))
            link(nc.vector.tensor_tensor(wres[:, 1, :], wres[:, 0, :], wpart[:, 1, :], ALU.subtract))
            link(nc.vector.tensor_copy(wpart[:, 2, :], wres[:, 1, :]))
            for j in range(3):
                nc.vector.tensor_tensor(wsl[:, :, j, :], sel[:, :, 1, :], nt(wpart[:, j, :]),
                                        ALU.mult).then_inc(s_wsl, 1)
            link(nc.vector.tensor_copy(tab[:, 0:2, :].rearrange("p g t -> p (g t)"), ps_small[:, 256:256 + 2 * NT]))
            link(nc.vector.tensor_scalar(tokf[:, 1, :], tab[:, 1, :], -1.0, 1.0, ALU.mult, ALU.add))
            link(nc.vector.scalar_tensor_tensor(out=tokf[:, 1, :], in0=tokf[:, 1, :], scalar=dump[:, 0:1],
                                                in1=tab[:, 0, :], op0=ALU.mult, op1=ALU.add))
            nc.vector.tensor_copy(sidx[:], tokf[:, 1, :]).then_inc(s_idx, 1)

            def slot_weights():
                dve.wait_ge(s_wtab, 1)
                link(nc.vector.tensor_copy(tab[:, 2:5, :].rearrange("p g t -> p (g t)"),
                                           ps_small[:, 320:320 + 3 * NT]))
                link(nc.vector.tensor_tensor(wslot[:, 0:NT], tab[:, 2, :], tab[:, 3, :], ALU.add))
                link(nc.vector.tensor_tensor(wslot[:, 0:NT], wslot[:, 0:NT], tab[:, 4, :], ALU.add))

            def lower_x(i, p):
                dve.wait_ge(s_xh, i + 1)
                nc.vector.tensor_tensor(xlT_sb[p], ps_h[:, 0:H], xhT_sb[p].bitcast(F32),
                                        ALU.subtract).then_inc(s_xts, 1)

            def hidden(i, p):
                dve.wait_ge(s_si, i + 1)
                nc.vector.tensor_tensor(h_sb[p], sg_sb[p], ps_scores[p][:, 1, :], ALU.mult).then_inc(s_hm, 1)

            def scale_y(i, p, first=False):
                dve.wait_ge(s_y, i + 1)
                if not first:
                    dve.wait_ge(s_add, 16 * i - 16)
                nc.vector.tensor_scalar(y_sb[p], ps_tr[:, 0:H], wslot[:, bass.ds(i, 1)], None,
                                        ALU.mult).then_inc(s_ys, 1)

            lower_x(0, 0)
            slot_weights()
            split(1)
            hidden(0, 0)
            lower_x(1, 1)
            split(2)
            hidden(1, 1)
            lower_x(2, 0)
            scale_y(0, 0, True)
            split(3)
            hidden(2, 0)
            lower_x(3, 1)
            scale_y(1, 1, True)
            with dve.Fori(2, E // 2) as pair:
                for p in range(2):
                    e = 2 * pair + p
                    split(e)
                    hidden(e - 1, 1 - p)
                    lower_x(e, p)
                    scale_y(e - 2, p)
            with dve.Fori(E - 2, NT - 3, 2) as i:
                for p in range(2):
                    hidden(i + p + 1, 1 - p)
                    lower_x(i + p + 2, p)
                    scale_y(i + p, p)
            hidden(NT - 2, 1)
            lower_x(NT - 1, 0)
            scale_y(NT - 3, 0)
            hidden(NT - 1, 0)
            scale_y(NT - 2, 1)
            scale_y(NT - 1, 0)

        @block.tensor
        def _(pe):
            def warm_up(n):
                for _ in range(n):
                    nc.tensor.matmul(ps_ht[:, :], ones_b[:], ones_b[:, :].unsqueeze(1).to_broadcast([P, 4, P]),
                                     start=True, stop=True)

            pe.wait_ge(s_ones, 1)
            warm_up(20)
            pe.wait_ge(s_const, 11)

            def turn_qk(b):
                pe.wait_ge(s_xn, b + 1)
                pe.wait_ge(s_c[0 if b < GROUPS[0][1] else 1], 16)
                if b >= 2:
                    pe.wait_ge(s_qks, b - 1)
                for c in range(KC):
                    nc.tensor.transpose(ps_scores[0][:, b % 2, c * P:(c + 1) * P],
                                        xn_sb[:, b, c * P:(c + 1) * P], ident[:])
                for c in range(KC):
                    last = nc.tensor.transpose(ps_scores[0][:, b % 2, (KC + c) * P:(KC + c + 1) * P],
                                               ctx_sb[:, b, c * P:(c + 1) * P], ident[:])
                last.then_inc(s_qkt, 1)

            def gates_of(b):
                pe.wait_ge(s_qks, b + 1)
                if b == 0:
                    pe.wait_ge(s_par2, 1)
                if b == 7:
                    pe.wait_ge(s_gT, 1)
                for c in range(2 * KC):
                    last = nc.tensor.matmul(gate_cols(b, S), wg_sb[:, c, :], qkT[:, b, c, :],
                                            start=(c == 0), stop=(c == 2 * KC - 1))
                last.then_inc(s_gate, 1)

            def turn_gates(i):
                b0, b1 = GROUPS[i]
                pe.wait_ge(s_gT, 1 + 2 * i)
                if i == 1:
                    pe.wait_ge(s_gsb, 1)
                for c0, c1, part in gT_parts[i:2 * i + 1]:
                    for b in range(c0, c1):
                        last = nc.tensor.transpose(ps_small[:, b * G2:(b + 1) * G2],
                                                   part[0:G2, (b - c0) * S:(b - c0 + 1) * S], ident[0:G2, 0:G2])
                last.then_inc(s_gt, 1)

            def cumsum(i):
                pe.wait_ge(s_logf, i + 1)
                if i == 1:
                    pe.wait_ge(s_ml, 1)
                b0, b1 = GROUPS[i]
                nc.tensor.matmul(ps_ht[:, ht_at[i]:ht_at[i] + GBH[i]], tri[:], logf[:, b0 * NH:b1 * NH],
                                 start=True, stop=True).then_inc(s_fps, 1)

            def turn_a(i):
                b0, b1 = GROUPS[i]
                pe.wait_ge(s_a, i + 1)
                at = ht_at[i] + GBH[i]
                nc.tensor.transpose(ps_ht[0:GBH[i], at:at + S], amat[:, b0 * NH:b1 * NH], ident[:]).then_inc(s_aT, 1)

            def turn_m(i):
                pe.wait_ge(s_mT, i + 1)
                at = ht_at[i] + GBH[i] + S
                nc.tensor.transpose(ps_ht[:, at:at + GBH[i]], mT[i][:], ident[0:GBH[i], 0:GBH[i]]).then_inc(s_m2, 1)

            def scores(b, c):
                if c == 0:
                    pe.wait_ge(s_qbd[b % 2], 16 * HC * (b // 2 + 1))
                if b >= 1:
                    pe.wait_ge(s_cm, KC * (b - 1) + c + 1)
                elif c == 1:
                    pe.wait_ge(s_gT, 3)
                for half in range(2):
                    rhs = qbd[:, b % 2, c, half * 4:(half + 1) * 4, :].rearrange("p h s -> p (h s)")
                    last = nc.tensor.matmul(ps_scores[c][:, half, :], qkT[:, b, KC + c, :], rhs, start=True, stop=True)
                last.then_inc(s_sc, 1)

            def cv(b, c):
                pe.wait_ge(s_cm, KC * b + c + 1)
                if c == 0:
                    pe.wait_ge(s_vp, b + 1)
                    if b >= 1:
                        pe.wait_ge(s_ots, b)
                    else:
                        pe.wait_ge(s_ml, 2)
                for h in range(c * HC, (c + 1) * HC):
                    g, j = h // 4, h % 4
                    last = nc.tensor.matmul(ps_ht[j * VW:(j + 1) * VW, g * P:(g + 1) * P], vp[:, b % 2, h, :],
                                            dec[:, b % 3, h, :], start=True, stop=True, tile_position=(0, j * VW))
                last.then_inc(s_cv, 1)

            def turn_cv(b):
                pe.wait_ge(s_ots, b + 1)
                if b >= 1:
                    pe.wait_ge(s_hst, b)
                for g in range(4):
                    last = nc.tensor.transpose(ps_h[:, g * P:(g + 1) * P], cvT[:, g * P:(g + 1) * P], ident[:])
                last.then_inc(s_ho, 1)

            def turn_x2(g):
                pe.wait_ge(s_xn2, 2 * g + 2)
                if g >= 1:
                    pe.wait_ge(s_rts, g)
                for j in range(2 * KC):
                    b, c = 2 * g + j // KC, j % KC
                    last = nc.tensor.transpose(ps_tr[:, j * P:(j + 1) * P], xn_sb[:, b, c * P:(c + 1) * P], ident[:])
                last.then_inc(s_rt, 1)

            def logits(g):
                pe.wait_ge(s_rts, g + 1)
                for j in range(2 * KC):
                    b, c = 2 * g + j // KC, j % KC
                    last = nc.tensor.matmul(ps_small[:, b * E:(b + 1) * E], xlT[:, j * P:(j + 1) * P], wr_sb[:, c, :],
                                            start=(c == 0), stop=(c == KC - 1))
                last.then_inc(s_lg, 1)

            def route(g):
                turn_x2(g)
                logits(g)

            for b in range(2):
                turn_qk(b)
            for b in range(3):
                gates_of(b)
                turn_qk(b + 2)
            turn_gates(0)
            gates_of(3)
            turn_qk(5)
            cumsum(0)
            gates_of(4)
            turn_a(0)
            turn_qk(6)
            turn_m(0)
            gates_of(5)
            turn_qk(7)
            gates_of(6)
            gates_of(7)
            scores(0, 0)
            turn_gates(1)
            cumsum(1)
            turn_a(1)
            turn_m(1)
            for b in range(B):
                if b >= 1:
                    scores(b, 0)
                    turn_cv(b - 1)
                scores(b, 1)
                cv(b, 0)
                if b == B - 1:
                    turn_x2(0)
                cv(b, 1)
                if b == B - 1:
                    logits(0)
            turn_cv(B - 1)
            route(1)
            warm_up(20)
            for g in range(2, NG):
                route(g)

            pe.wait_ge(s_mask, 1)
            NR = B * E
            rank = ps_small[:, 128:128 + NR]
            mk = mask.rearrange("p b e -> p (b e)")
            nc.tensor.matmul(rank, tri_s[:], mk, start=True, stop=True)
            for i in range(B - 1):
                nc.tensor.matmul(rank[:, (i + 1) * E:], ones_b[:],
                                 mask[:, i:i + 1, :].to_broadcast([P, B - 1 - i, E]),
                                 start=False, stop=True, skip_group_check=True)
            for i in range(B):
                last = nc.tensor.matmul(ps_small[:, 192:192 + E], ones_b[:], mk[:, i * E:(i + 1) * E],
                                        start=(i == 0), stop=(i == B - 1), skip_group_check=True)
            last.then_inc(s_rank, 1)
            for n in range(NS):
                if n % (NS // 4) == 0:
                    pe.wait_ge(s_sel, n // (NS // 4) + 2)
                last = nc.tensor.matmul(ps_small[:, 256:256 + 2 * NT], oh_r[:, n, :],
                                        sel[:, n].rearrange("p g t -> p (g t)"), start=(n == 0), stop=(n == NS - 1))
            last.then_inc(s_tab, 1)

            def weight_table():
                pe.wait_ge(s_wsl, 3)
                pe.wait_ge(s_idx, 1)
                for n in range(NS):
                    last = nc.tensor.matmul(ps_small[:, 320:320 + 3 * NT], oh_r[:, n, :],
                                            wsl[:, n].rearrange("p g t -> p (g t)"), start=(n == 0), stop=(n == NS - 1))
                last.then_inc(s_wtab, 1)

            def turn_x(i, slot_sem, n, p3, xts=None):
                pe.wait_ge(slot_sem, n)
                if xts is not None:
                    pe.wait_ge(s_xts, xts)
                for c in range(KC):
                    last = nc.tensor.transpose(ps_h[:, c * P:(c + 1) * P], xg_sb[p3][:, c * P:(c + 1) * P], ident[:])
                last.then_inc(s_xt, 1)

            def expert_of(i):
                return pe.value_load(eti[0:1, bass.ds(i, 1)], min_val=0, max_val=E - 1)

            def gate_up(i, p, e, split=True):
                pe.wait_ge(s_xts, i + 1)
                for n in range(2):
                    for k in range(KC):
                        xh, xl = (t[p][:, k * P:(k + 1) * P] for t in (xhT_sb, xlT_sb))
                        wh = arena_r[:, bass.ds(e * W13 + (n * KC + k) * I, I)]
                        wl = w13_r[:, bass.ds(e * W13 + (n * KC + k) * I, I)]
                        if split is not None:
                            pe.wait_ge(s_wl, SPLIT * split + n * KC + k + 1)
                        for j, (a, w) in enumerate(((xh, wl), (xl, wh), (xh, wh))):
                            last = nc.tensor.matmul(ps_scores[p][:, n, :], a, w, start=(k == 0 and j == 0),
                                                    stop=(k == KC - 1 and j == 2))
                last.then_inc(s_gu, 1)

            def turn_h(i, p, hts=True):
                pe.wait_ge(s_hm, i + 1)
                if hts:
                    pe.wait_ge(s_hts, i)
                for c in range(IC):
                    last = nc.tensor.transpose(ps_ht[:, c * P:(c + 1) * P], h_sb[p][:, c * P:(c + 1) * P], ident[:])
                last.then_inc(s_htp, 1)

            def down(i, p, e, ys=True):
                pe.wait_ge(s_hts, i + 1)
                if ys:
                    pe.wait_ge(s_ys, i)
                for k in range(IC):
                    last = nc.tensor.matmul(ps_tr[:, 0:H], hT_sb[p][:, k * P:(k + 1) * P],
                                            w2_sb[:, bass.ds(e * W2 + k * H, H)],
                                            start=(k == 0), stop=(k == IC - 1))
                last.then_inc(s_y, 1)

            pe.wait_ge(s_w[0], 16 * 3 * (E - LATE))
            pe.wait_ge(s_w[1], 16 * 3 * LATE)
            pe.wait_ge(s_eti, 1)
            def tile_step(i, p, q, split=None):
                e, e_before = expert_of(i), expert_of(i - 1)
                turn_h(i - 1, 1 - p)
                gate_up(i, p, e, split)
                j = (q + 1) % GATHER
                turn_x(i + 1, s_xg[j], 4 * (i + 1 - j) + 16, j, i + 1)
                down(i - 1, 1 - p, e_before)

            warm_up(8)
            turn_x(0, s_xg[0], 16, 0)
            weight_table()
            gate_up(0, 0, expert_of(0), 0)
            turn_x(1, s_xg[1], 16, 1, 1)
            turn_h(0, 0, False)
            gate_up(1, 1, expert_of(1), 1)
            turn_x(2, s_xg[2], 16, 2, 2)
            down(0, 0, expert_of(0), False)
            for i in range(2, E):
                tile_step(i, i % 2, i % GATHER, i)
            with pe.Fori(E, NT - 3, GATHER) as i:
                for q in range(GATHER):
                    tile_step(i + q, q % 2, q)
            for i in range(NT - 3, NT - 1):
                tile_step(i, i % 2, i % GATHER)
            turn_h(NT - 2, 1)
            gate_up(NT - 1, 0, expert_of(NT - 1), None)
            down(NT - 2, 1, expert_of(NT - 2))
            turn_h(NT - 1, 0)
            down(NT - 1, 0, expert_of(NT - 1))


_INS = ['x', 'ctx_2048', 'g_xattn', 'g_ffn', 'L0_xattn_Wi', 'L0_xattn_bi', 'L0_xattn_Wf', 'L0_xattn_bf',
        'L0_xattn_ln_scale', 'L0_ffn_w_gate', 'L0_ffn_w1', 'L0_ffn_w3', 'L0_ffn_w2']


def kernel(**inputs):
    import numpy as _np
    import concourse.bacc as _bacc
    from concourse import mybir as _mybir
    from concourse.bass_utils import run_bass_kernel_spmd as _run

    nc = _bacc.Bacc("TRN2", target_bir_lowering=False, num_devices=1)
    arrays, args = {}, []
    for name in _INS:
        a = _np.ascontiguousarray(inputs[name])
        arrays[f"in_{name}_dram"] = a
        args.append(nc.dram_tensor(f"in_{name}_dram", a.shape, _mybir.dt.from_np(a.dtype), kind="ExternalInput").ap())
    b, s, h = inputs['x'].shape
    args.append(nc.dram_tensor("out_0_dram", (b * s + 128, h), F32, kind="ExternalOutput").ap())
    bass_gated_mlstm_moe_kernel(nc, *args)
    r = _run(nc, [arrays], core_ids=[0])
    return r.results[0]["out_0_dram"][:b * s].reshape(b, s, h)
```
